# Optimizing a Trainium2 kernel written in Bass

```python
import numpy as np
import jax
import jax.numpy as jnp

def _softmax(x, axis=-1):
    return jax.nn.softmax(x, axis=axis)

def _gelu(x):
    return jax.nn.gelu(x, approximate=True)

def _silu(x):
    return jax.nn.silu(x)

def _sigmoid(x):
    return jax.nn.sigmoid(x)

def _layernorm(x, axis=-1, eps=1e-05):
    m = jnp.mean(x, axis=axis, keepdims=True)
    v = jnp.var(x, axis=axis, keepdims=True)
    return (x - m) / jnp.sqrt(v + eps)

def _scatter_add(tgt, idx, src, axis=0):
    return tgt.at[idx].add(src)

def _segment_sum(src, seg, n):
    return jax.ops.segment_sum(src, seg, n)
kernel_name = 'mk_macaron_d1_jaxref_r8_d78b7c'

def setup_inputs(seed: int=0):
    np.random.seed(seed)
    _w = jnp.asarray

    def _L0_attn_setup():
        import jax, jax.numpy as jnp
        import numpy as np
        NUM_HEADS = 16

        def _l2_normalize_complex(z):
            n = jnp.sqrt(jnp.sum(jnp.abs(z) ** 2, axis=-1, keepdims=True))
            return z / n
        key = jax.random.key(seed)
        k1, k2, k3, k4 = jax.random.split(key, 4)
        B, S, D = (4, 512, 256)
        scale = 1.0 / np.sqrt(D)
        return {'x': jax.random.normal(k1, (B, S, D), dtype=jnp.float32), 'W_q': jax.random.normal(k2, (D, D), dtype=jnp.float32) * scale, 'W_kv': jax.random.normal(k3, (D, D), dtype=jnp.float32) * scale, 'W_o': jax.random.normal(k4, (D, D), dtype=jnp.float32) * scale}
    _L0_attn_in = _L0_attn_setup()

    def _L0_ffn_setup():
        import jax, jax.numpy as jnp
        import numpy as np
        B, S, D = (4, 256, 256)
        E, F, K = (8, 128, 2)
        SF = 128
        EPS = 1e-06

        def _rmsnorm(x, w, eps=EPS):
            var = jnp.mean(x * x, axis=-1, keepdims=True)
            return x * jax.lax.rsqrt(var + eps) * w
        key = jax.random.key(seed)
        ks = jax.random.split(key, 9)
        g = lambda k, shape, scale: jax.random.normal(k, shape, jnp.float32) * scale
        return {'x': g(ks[0], (B, S, D), 1.0), 'rms_weight': jnp.ones((D,), jnp.float32), 'router_w': g(ks[1], (D, E), 0.02), 'w_gate': g(ks[2], (E, D, F), 0.02), 'w_up': g(ks[3], (E, D, F), 0.02), 'w_down': g(ks[4], (E, F, D), 0.02), 'sw_gate': g(ks[5], (D, SF), 0.02), 'sw_up': g(ks[6], (D, SF), 0.02), 'sw_down': g(ks[7], (SF, D), 0.02)}
    _L0_ffn_in = _L0_ffn_setup()
    _d = {'L0_attn_x': _L0_attn_in['x'], 'L0_attn_W_q': _L0_attn_in['W_q'], 'L0_attn_W_kv': _L0_attn_in['W_kv'], 'L0_attn_W_o': _L0_attn_in['W_o'], 'L0_ffn_rms_weight': _L0_ffn_in['rms_weight'], 'L0_ffn_router_w': _L0_ffn_in['router_w'], 'L0_ffn_w_gate': _L0_ffn_in['w_gate'], 'L0_ffn_w_up': _L0_ffn_in['w_up'], 'L0_ffn_w_down': _L0_ffn_in['w_down'], 'L0_ffn_sw_gate': _L0_ffn_in['sw_gate'], 'L0_ffn_sw_up': _L0_ffn_in['sw_up'], 'L0_ffn_sw_down': _L0_ffn_in['sw_down']}
    _x0 = _d['L0_attn_x']
    _d['L0_attn_x'] = jax.random.normal(jax.random.fold_in(jax.random.key(seed), 1), (2, 2048, 256), dtype=_x0.dtype)
    del _x0
    return _d

def reference(L0_attn_x, L0_attn_W_q, L0_attn_W_kv, L0_attn_W_o, L0_ffn_rms_weight, L0_ffn_router_w, L0_ffn_w_gate, L0_ffn_w_up, L0_ffn_w_down, L0_ffn_sw_gate, L0_ffn_sw_up, L0_ffn_sw_down):

    def _L0_attn_ref(x, W_q, W_kv, W_o):
        import jax, jax.numpy as jnp
        import numpy as np
        NUM_HEADS = 16

        def _l2_normalize_complex(z):
            n = jnp.sqrt(jnp.sum(jnp.abs(z) ** 2, axis=-1, keepdims=True))
            return z / n
        B, S, D = x.shape
        H = NUM_HEADS
        hd = D // H
        q = (x @ W_q.T).reshape(B, S, H, hd)
        kv = (x @ W_kv.T).reshape(B, S, H, hd)
        qf = jnp.fft.fft(q, axis=-1)
        kvf = jnp.fft.fft(kv, axis=-1)
        qf = _l2_normalize_complex(qf)
        kvf = _l2_normalize_complex(kvf)
        kvf = jnp.cumsum(kvf, axis=1)
        qv = qf * kvf
        values_hat = jnp.fft.ifft(qv, axis=-1).real.astype(x.dtype)
        values_hat = values_hat.reshape(B, S, D)
        return values_hat @ W_o.T

    def _L0_ffn_ref(x, rms_weight, router_w, w_gate, w_up, w_down, sw_gate, sw_up, sw_down):
        import jax, jax.numpy as jnp
        import numpy as np
        B, S, D = (4, 256, 256)
        E, F, K = (8, 128, 2)
        SF = 128
        EPS = 1e-06

        def _rmsnorm(x, w, eps=EPS):
            var = jnp.mean(x * x, axis=-1, keepdims=True)
            return x * jax.lax.rsqrt(var + eps) * w
        b, s, d = x.shape
        e = router_w.shape[1]
        h = _rmsnorm(x, rms_weight)
        ht = h.reshape(-1, d)
        t = ht.shape[0]
        logits = ht @ router_w
        probs = jax.nn.softmax(logits, axis=-1)
        topv, topi = jax.lax.top_k(probs, K)
        topv = topv / jnp.sum(topv, axis=-1, keepdims=True)
        w_dense = jnp.zeros((t, e), ht.dtype).at[jnp.arange(t)[:, None], topi].set(topv)
        g = jnp.einsum('td,edf->tef', ht, w_gate)
        u = jnp.einsum('td,edf->tef', ht, w_up)
        eo = jnp.einsum('tef,efd->ted', jax.nn.silu(g) * u, w_down)
        moe = jnp.einsum('te,ted->td', w_dense, eo)
        sh = jax.nn.silu(ht @ sw_gate) * (ht @ sw_up) @ sw_down
        return (moe + sh).reshape(b, s, d)
    x = L0_attn_x
    x = x + 0.5 * _L0_ffn_ref(_layernorm(x, axis=-1), L0_ffn_rms_weight, L0_ffn_router_w, L0_ffn_w_gate, L0_ffn_w_up, L0_ffn_w_down, L0_ffn_sw_gate, L0_ffn_sw_up, L0_ffn_sw_down)
    x = x + _L0_attn_ref(_layernorm(x, axis=-1), L0_attn_W_q, L0_attn_W_kv, L0_attn_W_o)
    x = x + 0.5 * _L0_ffn_ref(_layernorm(x, axis=-1), L0_ffn_rms_weight, L0_ffn_router_w, L0_ffn_w_gate, L0_ffn_w_up, L0_ffn_w_down, L0_ffn_sw_gate, L0_ffn_sw_up, L0_ffn_sw_down)
    return x

_drawn_inputs = setup_inputs


def setup_inputs(seed=0):
    import zlib

    import numpy as np

    out = dict(_drawn_inputs(seed))
    spreads = {'L0_ffn_rms_weight': (1.0, 0.6)}
    factors = {'L0_ffn_router_w': 8.0,
     'L0_ffn_w_gate': 6.742,
     'L0_ffn_w_up': 6.656,
     'L0_ffn_w_down': 6.64,
     'L0_ffn_sw_gate': 4.511,
     'L0_ffn_sw_up': 3.996,
     'L0_ffn_sw_down': 4.268}
    for name, (base, spread) in spreads.items():
        noise = np.random.default_rng([zlib.crc32(name.encode()), seed]).standard_normal(out[name].shape)
        drawn = base * np.exp(spread * noise) if base else spread * noise
        out[name] = jnp.asarray(drawn.astype(out[name].dtype))
    for name, factor in factors.items():
        out[name] = (out[name] * factor).astype(out[name].dtype)
    return out
```

```python
from contextlib import ExitStack

import numpy as np

import concourse.bass as bass
from concourse import mybir

ALU = mybir.AluOpType
ACT = mybir.ActivationFunctionType
AX = mybir.AxisListType
F32 = mybir.dt.float32
F32R = mybir.dt.float32r
I32 = mybir.dt.int32

P = 128
TOK = 512
NT = TOK // P
D = 256
KD = D // P
E = 8
NE = E + 1
F = 128
HEADS, HD = 16, 16
HB = HD // 2
LN_EPS, RMS_EPS = 1e-5, 1e-6
BIG = 3.0e38
RSQRT_MAGIC = 0x5F3759DF
CONV_SCALE = 1.0 / (2.0 * float(np.sqrt(HD / 2)))

WG, WU, WD, WCOLS = 0, 2 * F, 4 * F, 4 * F + D

C_ID, C_SELN, C_SELB, C_RANK, C_SIGN, C_ONE = 0, 128, 192, 448, 456, 457
C_DFT = 458
C_COLS = C_DFT + KD * D

STAGES_A = [
    (["loadx"], []),
    ([], ["stat1"]),
    (["ycopy1"], ["norm1"]),
    (["sum1"], ["statA", "turn1"]),
    (["route1", "xa"], ["normA", "turnA"]),
    (["gatew1"], ["wrow1", "q"]),
    ([], ["k"]),
    ([], ["sq"]),
    (["wspread1"], ["inv"]),
]
STAGES_B = [
    (["spread"], []),
    ([], ["conv"]),
    (["ycopy2"], ["osplit"]),
    (["sum2"], []),
    (["wo"], []),
    (["sum3"], ["stat2", "xc"]),
    (["norm2"], ["turn2"]),
    ([], ["route2"]),
    (["gatew2"], ["wrow2", "wspread2"]),
]
SIDE = {"turn1", "route1", "wrow1", "turnA", "q", "k", "sq", "inv", "spread", "wo", "sum3",
        "turn2", "route2", "wrow2", "sum1", "sum2"}
NORMS = ("norm1", "normA", "norm2")


def stages(i, table, groups):
    gone = set()
    if type(i) is int and i == 0:
        gone |= {"ycopy2", "sum2"}
    if type(i) is int and i == groups - 1:
        gone |= {"loadx", "stat1", "norm1", "turn1", "route1", "gatew1", "wrow1", "wspread1", "xa"}
    return [tuple([s for s in part if s not in gone] for part in step) for step in table]


def period_side(i, groups):
    per, first = len(order(1, SIDE, groups)), len(SETUP_SIDE)
    if type(i) is int and i == 0:
        return first
    if type(i) is int and i == groups:
        return period_side(groups - 1, groups) + len(order(groups - 1, SIDE, groups))
    return per * i + (first + len(order(0, SIDE, groups)) - per)


def order(i, names, groups):
    return [s for step in stages(i, STAGES_A, groups) + stages(i, STAGES_B, groups)
            for part in step for s in part if s in names]


SETUP_SIDE = ["turn1", "route1", "wrow1", "wq", "wk", "woT", "wo"]


def side_no(i, name, groups):
    if type(i) is int and i == -1:
        return SETUP_SIDE.index(name)
    if type(i) is int and i == groups:
        return period_side(i, groups)
    return period_side(i, groups) + order(i, SIDE, groups).index(name)


def norm_no(i, name, groups):
    if type(i) is int and i == -1:
        return 0
    return 3 * i + 1 + order(i, NORMS, groups).index(name)


def constants():
    c = np.zeros((P, C_COLS), np.float32)
    p = np.arange(P)
    c[p, C_ID + p] = 1.0
    c[p, C_SELN + p // HB] = 1.0
    c[p, C_SELN + 32 + HEADS + p // HB] = 1.0
    for m in range(P):
        c[m // HB, C_SELB + m] = 1.0
        c[HEADS + m // HB, C_SELB + P + m] = 1.0
    c[:, C_RANK:C_RANK + E] = E - np.arange(E)
    c[:, C_SIGN] = np.where(p % HB == 0, 1.0, -1.0)
    c[:, C_ONE] = 1.0
    n = np.arange(HD)
    basis = np.zeros((2, HB, HD))
    basis[0, 0] = np.sqrt(2.0 / HD) * (n % 2 == 0)
    basis[1, 0] = np.sqrt(2.0 / HD) * (n % 2 == 1)
    for k in range(1, HB):
        basis[0, k] = np.sqrt(2.0 / HD) * np.cos(2 * np.pi * k * n / HD)
        basis[1, k] = -np.sqrt(2.0 / HD) * np.sin(2 * np.pi * k * n / HD)
    full = np.zeros((D, D), np.float32)
    for h in range(HEADS):
        for plane in range(2):
            for k in range(HB):
                full[h * HD:(h + 1) * HD, plane * P + h * HB + k] = basis[plane, k]
    c[:, C_DFT:] = full.reshape(KD, P, D).transpose(1, 0, 2).reshape(P, KD * D)
    return c


def build(nc, x, W_q, W_kv, W_o, rms_weight, router_w, w_gate, w_up, w_down,
          sw_gate, sw_up, sw_down, consts, row_dram, out):
    B, S, _ = x.shape
    GROUPS = B * S // TOK
    PER_SEQ = S // TOK
    LAST = GROUPS - 1
    assert x.shape[2] == D and PER_SEQ == 4 and S % TOK == 0

    x_rows = x.rearrange("b s d -> (b s) d")
    out_rows = out.rearrange("b s d -> (b s) d")

    with ExitStack() as ctx:
        def sb(name, shape, dt=F32):
            return ctx.enter_context(nc.sbuf_tensor(name, shape, dt))

        def sem(name):
            return ctx.enter_context(nc.semaphore(name))

        gate_ps = ctx.enter_context(nc.psum_tensor("gate_ps", [P, 2, TOK], F32))
        up_ps = ctx.enter_context(nc.psum_tensor("up_ps", [P, 2, TOK], F32))
        y_ps = ctx.enter_context(nc.psum_tensor("y_ps", [P, KD, TOK], F32))
        side = ctx.enter_context(nc.psum_tensor("side", [P, 2, TOK], F32))

        w_raw = sb("w_raw", [P, 3, WCOLS])
        w_hi = sb("w_hi", [P, NE, WCOLS], F32R)
        w_lo = sb("w_lo", [P, NE, WCOLS], F32R)
        router = sb("router", [P, KD, E])
        router_hi = sb("router_hi", [P, KD, E], F32R)
        router_lo = sb("router_lo", [P, KD, E], F32R)
        rmsw = sb("rmsw", [P, KD])
        cst = sb("cst", [P, C_COLS])
        qk_hi = sb("qk_hi", [P, 2, KD, D], F32R)
        qk_lo = sb("qk_lo", [P, 2, KD, D], F32R)
        wo_hi = sb("wo_hi", [P, 2, D], F32R)
        wo_lo = sb("wo_lo", [P, 2, D], F32R)

        x_next = sb("x_next", [P, NT, D])
        x_in = sb("x_in", [P, NT, D])
        x_mid = sb("x_mid", [P, NT, D])
        x_last = sb("x_last", [P, NT, D])
        xn = sb("xn", [P, NT, D])
        stats = sb("stats", [P, NT, 6])
        mv = sb("mv", [P, NT, 2])
        scl = sb("scl", [P, 8, NT])
        c_eps = sb("c_eps", [P, 4, NT])

        h_hi = {k: sb(f"h{k}_hi", [P, KD, TOK], F32R) for k in "1A2"}
        h_lo = {k: sb(f"h{k}_lo", [P, KD, TOK], F32R) for k in "1A2"}
        act = sb("act", [P, 3, TOK])
        act_hi = sb("act_hi", [P, 3, TOK], F32R)
        act_lo = sb("act_lo", [P, 3, TOK], F32R)
        yT = sb("yT", [P, KD, TOK])

        lg = sb("lg", [P, 6, NT, E])
        rt = sb("rt", [P, 8, NT])
        wt = sb("wt", [P, E, NT])
        wT = sb("wT", [E * NT, P])
        wrow = sb("wrow", [1, E * TOK])
        wb = sb("wb", [P, E, TOK])

        q_sb = sb("q_sb", [P, 2, TOK])
        k_sb = sb("k_sb", [P, 2, TOK])
        sq_q = sb("sq_q", [P, 2, TOK])
        sq_k = sb("sq_k", [P, 2, TOK])
        nrm = sb("nrm", [P, 4, P])
        invT = sb("invT", [2 * HEADS, TOK])
        carry = sb("carry", [P, 2, 2 * PER_SEQ + 2])
        o_sb = sq_q
        o_hi = sb("o_hi", [P, 2, TOK], F32R)
        o_lo = sb("o_lo", [P, 2, TOK], F32R)
        wq_raw, wk_raw, wo_raw, woT = q_sb, k_sb, sq_q, sq_k

        ident = cst[:, C_ID:C_ID + P]
        one = cst[:, C_ONE:C_ONE + 1]

        gate_done, up_done, down_done, silu_done = sem("gate_done"), sem("up_done"), sem("down_done"), sem("silu_done")
        prod_done, weighted, act_hi_done, act_lo_done = sem("prod_done"), sem("weighted"), sem("act_hi_done"), sem("act_lo_done")
        y_copied, side_full, side_read = sem("y_copied"), sem("side_full"), sem("side_read")
        stats_done, scale_done, norm_done, hi_done = sem("stats_done"), sem("scale_done"), sem("norm_done"), sem("hi_done")
        diff_done, tanh_done, wt_done, row_out = sem("diff_done"), sem("tanh_done"), sem("wt_done"), sem("row_out")
        wrow_in, wb_done = sem("wrow_in"), sem("wb_done")
        x_next_in, x_in_done, x1_done, x2_done = sem("x_next_in"), sem("x_in_done"), sem("x1_done"), sem("x2_done")
        x3_done, x_last_done, stored = sem("x3_done"), sem("x_last_done"), sem("stored")
        squared, sq_summed, inv_done, cum_done = sem("squared"), sem("sq_summed"), sem("inv_done"), sem("cum_done")
        cross_done, o_done, o_hi_done, o_lo_done = sem("cross_done"), sem("o_done"), sem("o_hi_done"), sem("o_lo_done")
        w_hi_done, w_lo_done, cst_in, small_in = sem("w_hi_done"), sem("w_lo_done"), sem("cst_in"), sem("small_in")
        attn_w_in, router_hi_done, router_split, filled = sem("attn_w_in"), sem("router_hi_done"), sem("router_split"), sem("filled")
        carried, dve_step, pool_step = sem("carried"), sem("dve_step"), sem("pool_step")
        raw_in = [sem(f"raw_in{r}") for r in range(3)]

        def positive(value):
            return type(value) is not int or value > 0

        def carry_wait(eng):
            eng.sem_inc(carried, 1)

        class Steps:

            def __init__(self, eng, sem, name):
                self.eng, self.sem, self.name, self.base, self.k = eng, sem, name, 0, 0

            def at(self, base):
                self.base, self.k = base, 0

            def mark(self, ins):
                ins.then_inc(self.sem, 1)
                self.k += 1
                return self.base + self.k

            def link(self, ins):
                self.eng.wait_ge(self.sem, self.mark(ins))

        def ffn_no(i, window):
            return 2 * i if window == "A" else 2 * i + 1

        def run_periods(eng, window, counted=()):
            def measured(i):
                before = [c.k for c in counted]
                window(i, "A")
                window(i, "B")
                return [c.k - b for c, b in zip(counted, before)]

            measured(0)
            starts = [c.base + c.k for c in counted]
            with eng.Fori(1, LAST) as i:
                for c, s in zip(counted, starts):
                    c.at((i - 1) * STEPS[c.name] + s)
                per = measured(i)
                assert per == [STEPS[c.name] for c in counted], per
            for c, s in zip(counted, starts):
                c.at(s + STEPS[c.name] * (LAST - 1))
            measured(LAST)

        STEPS = {"dve_step": 47, "pool_step": 13}

        def pending(i):
            return not (type(i) is int and i == 0)

        def route_no(i, name):
            if type(i) is int and i == -1:
                return 0
            if name[-1] == "1":
                return 2 * i + 1
            return 2 * i + 2 - (type(i) is int and i == LAST)

        def sum_no(i, name):
            if type(i) is int and i in (0, GROUPS):
                return 0 if i == 0 else 2 * GROUPS - 1
            return 2 * i - 1 if name[-1] == "1" else 2 * i

        def has_ffn(i, w):
            return not (type(i) is int and ((w == "A" and i == 0) or (w == "B" and i == LAST)))

        block = ctx.enter_context(nc.Block())

        @block.sync
        def _(sp):
            def load_expert(e):
                if e >= 3:
                    sp.wait_ge(w_lo_done, e - 2)
                g, u, d = (sw_gate, sw_up, sw_down) if e == 0 else (w_gate[e - 1], w_up[e - 1], w_down[e - 1])
                r = e % 3
                sp.dma_start(w_raw[:, r, WG:WU].rearrange("p (k f) -> p k f", k=KD),
                             g.rearrange("(k p) f -> p k f", p=P)).then_inc(raw_in[r], 16)
                sp.dma_start(w_raw[:, r, WU:WD].rearrange("p (k f) -> p k f", k=KD),
                             u.rearrange("(k p) f -> p k f", p=P)).then_inc(raw_in[r], 16)
                sp.dma_start(w_raw[:, r, WD:], d).then_inc(raw_in[r], 16)

            def load_x(g):
                sp.dma_start(x_next[:], x_rows[bass.ds(g * TOK, TOK), :].rearrange("(t p) d -> p t d", p=P)
                             ).then_inc(x_next_in, 16)

            def stage(s, i):
                if s == "loadx":
                    sp.wait_ge(x_in_done, i + 1)
                    carry_wait(sp)
                    sp.wait_ge(norm_done, norm_no(i - 1, "norm1", GROUPS) + 1)
                    carry_wait(sp)
                    load_x(i + 1)
                if s in ("wrow1", "wrow2"):
                    sp.wait_ge(side_read, side_no(i, s, GROUPS) + 1)
                    carry_wait(sp)
                    if positive(E * route_no(i, s)):
                        sp.wait_ge(wb_done, E * route_no(i, s))
                    carry_wait(sp)
                    sp.dma_start(row_dram, wT[:, :]).then_inc(row_out, 16)
                    sp.wait_ge(row_out, 16 * (route_no(i, s) + 1))
                    carry_wait(sp)
                    sp.dma_start(wrow[:, :], row_dram.rearrange("(a r) c -> a (r c)", a=1)
                                 ).then_inc(wrow_in, 16)
                if s == "sum2":
                    sp.wait_ge(x3_done, i)
                    carry_wait(sp)
                    sp.dma_start(out_rows[bass.ds((i - 1) * TOK, TOK), :].rearrange("(t p) d -> p t d", p=P),
                                 x_last[:]).then_inc(stored, 16)

            load_x(0)
            sp.dma_start(cst[:], consts).then_inc(cst_in, 16)
            sp.dma_start(rmsw[:], rms_weight.rearrange("(k p) -> p k", p=P), allow_slow_non_contiguous=True).then_inc(small_in, 16)
            sp.dma_start(router[:], router_w.rearrange("(k p) e -> p k e", p=P)).then_inc(small_in, 16)
            for e in range(3):
                load_expert(e)
            for dst, src in ((wq_raw, W_q), (wk_raw, W_kv), (wo_raw, W_o)):
                sp.dma_start(dst[:, :, 0:D], src.rearrange("(k p) d -> p k d", p=P)).then_inc(attn_w_in, 16)
            stage("wrow1", -1)
            for e in range(3, NE):
                load_expert(e)

            def window(i, w):
                for before, after in stages(i, STAGES_A if w == "A" else STAGES_B, GROUPS):
                    for s in before + after:
                        stage(s, i)

            run_periods(sp, window)
            stage("sum2", GROUPS)
            sp.wait_ge(stored, 16 * GROUPS)

        @block.tensor
        def _(pe):
            def triple(dst, a, b, start, stop):
                (ah, al), (bh, bl) = a, b
                nc.tensor.matmul(dst, ah, bh, start=start, stop=False, skip_group_check=True)
                nc.tensor.matmul(dst, ah, bl, start=False, stop=False, skip_group_check=True)
                return nc.tensor.matmul(dst, al, bh, start=False, stop=stop, skip_group_check=True)

            def gate_up(f, e, kind):
                n = NE * f + e
                if type(f) is int and f == 0:
                    pe.wait_ge(w_hi_done, e + 1)
                    pe.wait_ge(w_lo_done, e + 1)
                last = n - (1 if e == 0 else 3 if e == 1 else 2)
                if positive(last + 1):
                    pe.wait_ge(silu_done, last + 1)
                for k in range(KD):
                    c = slice(WG + k * F, WG + (k + 1) * F)
                    ins = triple(gate_ps[:, e % 2], (w_hi[:, e, c], w_lo[:, e, c]),
                                 (h_hi[kind][:, k], h_lo[kind][:, k]), k == 0, k == KD - 1)
                ins.then_inc(gate_done, 1)
                if positive(last + 1):
                    pe.wait_ge(prod_done, last + 1)
                for k in range(KD):
                    c = slice(WU + k * F, WU + (k + 1) * F)
                    ins = triple(up_ps[:, e % 2], (w_hi[:, e, c], w_lo[:, e, c]),
                                 (h_hi[kind][:, k], h_lo[kind][:, k]), k == 0, k == KD - 1)
                ins.then_inc(up_done, 1)

            def down(f, e):
                n = NE * f + e
                pe.wait_ge(act_lo_done, n + 1)
                if e == 0:
                    if positive(f):
                        pe.wait_ge(y_copied, f)
                for m in range(KD):
                    c = slice(WD + m * P, WD + (m + 1) * P)
                    ins = triple(y_ps[:, m], (w_hi[:, e, c], w_lo[:, e, c]),
                                 (act_hi[:, e % 3], act_lo[:, e % 3]), e == 0, e == NE - 1)
                ins.then_inc(down_done, 1)

            def back(src):
                for t in range(NT):
                    for m in range(KD):
                        ins = nc.tensor.transpose(side[:, t // 2, (t % 2) * D + m * P:(t % 2) * D + (m + 1) * P],
                                                  src[:, m, t * P:(t + 1) * P], ident)
                return ins

            def stage(s, i):
                if s in SIDE:
                    u = side_no(i, s, GROUPS)
                    if s in ("turn1", "turnA", "turn2"):
                        pe.wait_ge(norm_done, norm_no(i, "norm" + s[-1], GROUPS) + 1)
                    if s in ("wrow1", "wrow2"):
                        pe.wait_ge(wt_done, route_no(i, s) + 1)
                    if s in ("sum1", "sum2"):
                        pe.wait_ge(y_copied, sum_no(i, s) + 1)
                    if s == "sq":
                        pe.wait_ge(sq_summed, 2 * i + 2)
                    if s == "inv":
                        pe.wait_ge(inv_done, i + 1)
                    if s == "wo":
                        pe.wait_ge(o_lo_done, i + 1)
                    if positive(u):
                        pe.wait_ge(side_read, u)
                if s in ("turn1", "turnA", "turn2"):
                    for k in range(KD):
                        for t in range(NT):
                            ins = nc.tensor.transpose(side[:, k, t * P:(t + 1) * P],
                                                      xn[:, t, k * P:(k + 1) * P], ident)
                elif s in ("route1", "route2"):
                    hh, hl = h_hi[s[-1]], h_lo[s[-1]]
                    for t in range(NT):
                        for k in range(KD):
                            c = slice(t * P, (t + 1) * P)
                            ins = triple(side[:, 0, t * E:(t + 1) * E], (hh[:, k, c], hl[:, k, c]),
                                         (router_hi[:, k], router_lo[:, k]), k == 0, k == KD - 1)
                elif s in ("wrow1", "wrow2"):
                    ins = nc.tensor.transpose(side[0:E * NT, 1, 0:P], wt[:].rearrange("p e t -> p (e t)"), ident)
                elif s in ("sum1", "sum2", "sum3"):
                    ins = back(yT)
                elif s in ("q", "k"):
                    j = "qk".index(s)
                    for plane in range(2):
                        for k in range(KD):
                            c = slice(plane * P, (plane + 1) * P)
                            ins = triple(side[:, plane], (qk_hi[:, j, k, c], qk_lo[:, j, k, c]),
                                         (h_hi["A"][:, k], h_lo["A"][:, k]), k == 0, k == KD - 1)
                elif s == "sq":
                    for t in range(NT):
                        dst = side[:, 0, 2 * HEADS * t:2 * HEADS * (t + 1)]
                        c = slice(t * P, (t + 1) * P)
                        nc.tensor.matmul(dst, sq_q[:, 0, c], cst[:, C_SELN:C_SELN + 32],
                                         start=True, stop=False, skip_group_check=True)
                        ins = nc.tensor.matmul(dst, sq_k[:, 0, c], cst[:, C_SELN + 32:C_SELN + 64],
                                               start=False, stop=True, skip_group_check=True)
                elif s == "inv":
                    for t in range(NT):
                        ins = nc.tensor.transpose(side[0:32, 1, t * P:(t + 1) * P],
                                                  nrm[:, 1, 32 * t:32 * (t + 1)], ident)
                elif s == "spread":
                    for j in range(2):
                        ins = nc.tensor.matmul(side[:, j], cst[0:32, C_SELB + j * P:C_SELB + (j + 1) * P],
                                               invT[:], start=True, stop=True)
                elif s == "wo":
                    for m in range(KD):
                        for plane in range(2):
                            c = slice(m * P, (m + 1) * P)
                            ins = triple(side[:, m], (wo_hi[:, plane, c], wo_lo[:, plane, c]),
                                         (o_hi[:, plane], o_lo[:, plane]), plane == 0, plane == 1)
                else:
                    return
                ins.then_inc(side_full, 1)

            def fold(name, raw):
                pe.wait_ge(side_read, SETUP_SIDE.index(name))
                pe.wait_ge(attn_w_in, 48)
                for m in range(KD):
                    for k in range(KD):
                        ins = nc.tensor.matmul(side[:, m, 0:D], raw[:, k, m * P:(m + 1) * P],
                                               cst[:, C_DFT + k * D:C_DFT + (k + 1) * D],
                                               start=k == 0, stop=k == KD - 1)
                ins.then_inc(side_full, 1)

            def turn_wo():
                pe.wait_ge(side_read, SETUP_SIDE.index("woT"))
                for m in range(KD):
                    for k in range(KD):
                        ins = nc.tensor.transpose(side[:, m, k * P:(k + 1) * P],
                                                  wo_raw[:, k, m * P:(m + 1) * P], ident)
                ins.then_inc(side_full, 1)

            def fold_wo():
                pe.wait_ge(side_read, SETUP_SIDE.index("wo"))
                for plane in range(2):
                    for k in range(KD):
                        c = C_DFT + k * D + plane * P
                        ins = nc.tensor.matmul(side[:, plane, 0:D], cst[:, c:c + P], woT[:, k, 0:D],
                                               start=k == 0, stop=k == KD - 1)
                ins.then_inc(side_full, 1)

            pe.wait_ge(cst_in, 16)
            stage("turn1", -1)
            pe.wait_ge(router_split, 1)
            stage("route1", -1)
            setup = {1: lambda: stage("wrow1", -1), 3: lambda: fold("wq", wq_raw), 4: lambda: fold("wk", wk_raw),
                     5: turn_wo, 6: fold_wo}
            for e in range(NE):
                gate_up(0, e, "1")
                if e == 0:
                    setup[1]()
                elif e in (3, 4, 5, 6):
                    setup[e]()
                if e >= 2:
                    down(0, e - 2)
            down(0, NE - 2)
            down(0, NE - 1)

            def window(i, w):
                f = ffn_no(i, w)
                table = stages(i, STAGES_A if w == "A" else STAGES_B, GROUPS)
                for e, (before, after) in enumerate(table):
                    if has_ffn(i, w):
                        gate_up(f, e, "2" if w == "A" else "1")
                    for s in before:
                        stage(s, i)
                    if e < 2 and pending(i):
                        down(f - 1, NE - 2 + e)
                    elif e >= 2 and has_ffn(i, w):
                        down(f, e - 2)
                    for s in after:
                        stage(s, i)

            run_periods(pe, window)
            f = 2 * GROUPS - 1
            for e in range(NE):
                gate_up(f, e, "2")
                if e >= 2:
                    down(f, e - 2)
            down(f, NE - 2)
            down(f, NE - 1)
            stage("sum2", GROUPS)

        @block.scalar
        def _(act_e):
            A = nc.scalar

            def silu(f, e):
                n = NE * f + e
                act_e.wait_ge(gate_done, n + 1)
                if positive(n - 2):
                    act_e.wait_ge(act_lo_done, n - 2)
                A.activation(act[:, e % 3], gate_ps[:, e % 2], ACT.Silu).then_inc(silu_done, 1)

            def high(f, e):
                n = NE * f + e
                if e == 0:
                    act_e.wait_ge(prod_done, n + 1)
                else:
                    act_e.wait_ge(weighted, E * f + e)
                if positive(n - 2):
                    act_e.wait_ge(down_done, n - 2)
                A.activation(act_hi[:, e % 3], act[:, e % 3], ACT.Copy).then_inc(act_hi_done, 1)

            def core(f, e, first):
                silu(f, e)
                if e >= 1:
                    high(f, e - 1)
                elif not first:
                    high(f - 1, NE - 1)

            def stage(s, i):
                full = side_no(i, s, GROUPS) + 1 if s in SIDE else None
                if s in ("turn1", "turnA", "turn2"):
                    kind = s[-1]
                    act_e.wait_ge(side_full, full)
                    for k in range(KD):
                        if kind == "A":
                            ins = A.activation(h_hi[kind][:, k], side[:, k], ACT.Copy)
                        else:
                            ins = A.activation(h_hi[kind][:, k], side[:, k], ACT.Copy, scale=rmsw[:, k:k + 1])
                        ins.then_inc(hi_done, 1)
                elif s in ("gatew1", "gatew2"):
                    act_e.wait_ge(diff_done, route_no(i, s) + 1)
                    A.activation(rt[:, 5], rt[:, 4], ACT.Tanh, scale=0.5).then_inc(tanh_done, 1)
                elif s in ("wrow1", "wrow2"):
                    act_e.wait_ge(side_full, full)
                    if positive(16 * route_no(i, s)):
                        act_e.wait_ge(wrow_in, 16 * route_no(i, s))
                    A.copy(wT[:, :], side[0:E * NT, 1, 0:P]).then_inc(side_read, 1)
                elif s in ("ycopy1", "ycopy2"):
                    act_e.wait_ge(down_done, NE * (sum_no(i, s) + 1))
                    if s == "ycopy1":
                        act_e.wait_ge(side_read, period_side(i, GROUPS))
                    else:
                        act_e.wait_ge(x1_done, i + 1 if not (type(i) is int and i == GROUPS) else GROUPS)
                    A.activation(yT[:], y_ps[:], ACT.Copy, scale=0.5).then_inc(y_copied, 1)
                elif s == "xa":
                    act_e.wait_ge(x1_done, i + 1)
                    act_e.wait_ge(x_next_in, 16 * (i + 2))
                    A.copy(x_in[:], x_next[:]).then_inc(x_in_done, 1)
                elif s == "xc":
                    act_e.wait_ge(x2_done, i + 1)
                    if positive(16 * i):
                        act_e.wait_ge(stored, 16 * i)
                    A.copy(x_last[:], x_mid[:]).then_inc(x_last_done, 1)
                elif s in ("q", "k"):
                    act_e.wait_ge(side_full, full)
                    sq, dst = (sq_q, q_sb) if s == "q" else (sq_k, k_sb)
                    A.activation(sq[:], side[:], ACT.Square).then_inc(squared, 1)
                    A.copy(dst[:], side[:]).then_inc(side_read, 1)
                elif s == "inv":
                    act_e.wait_ge(side_full, full)
                    A.copy(invT[:, :], side[0:32, 1, :]).then_inc(side_read, 1)
                elif s == "osplit":
                    act_e.wait_ge(o_done, i + 1)
                    A.activation(o_hi[:], o_sb[:], ACT.Copy).then_inc(o_hi_done, 1)
                elif s == "wo":
                    act_e.wait_ge(side_full, full)
                    A.copy(yT[:], side[:]).then_inc(side_read, 1)

            def split_expert(e):
                act_e.wait_ge(raw_in[e % 3], 48 * (e // 3 + 1))
                A.activation(w_hi[:, e], w_raw[:, e % 3], ACT.Copy).then_inc(w_hi_done, 1)

            def setup_high(name, dst, scale):
                act_e.wait_ge(side_full, SETUP_SIDE.index(name) + 1)
                A.activation(dst, side[:, :, 0:D], ACT.Copy, scale=scale).then_inc(hi_done, 1)

            act_e.wait_ge(small_in, 32)
            A.activation(router_hi[:], router[:], ACT.Copy).then_inc(router_hi_done, 1)
            act_e.wait_ge(x_next_in, 16)
            A.copy(x_in[:], x_next[:]).then_inc(x_in_done, 1)
            stage("turn1", -1)
            split_expert(0)
            split_expert(1)
            for e in range(NE):
                core(0, e, True)
                if e + 2 < NE:
                    split_expert(e + 2)
                if e == 0:
                    stage("gatew1", -1)
                    stage("wrow1", -1)
                if e == 3:
                    setup_high("wq", qk_hi[:, 0], 1.0)
                if e == 4:
                    setup_high("wk", qk_hi[:, 1], 1.0)
                if e == 5:
                    act_e.wait_ge(side_full, SETUP_SIDE.index("woT") + 1)
                    A.copy(woT[:, :, 0:D], side[:, :, 0:D]).then_inc(side_read, 1)
                if e == 6:
                    setup_high("wo", wo_hi[:], CONV_SCALE)
            high(0, NE - 1)

            def window(i, w):
                f = ffn_no(i, w)
                for e, (before, after) in enumerate(stages(i, STAGES_A if w == "A" else STAGES_B, GROUPS)):
                    if has_ffn(i, w):
                        core(f, e, not pending(i))
                    elif e == 0 and pending(i):
                        high(f - 1, NE - 1)
                    for s in before + after:
                        stage(s, i)

            run_periods(act_e, window)
            f = 2 * GROUPS - 1
            for e in range(NE):
                core(f, e, True)
            high(f, NE - 1)
            stage("ycopy2", GROUPS)

        @block.vector
        def _(dve):
            V = nc.vector
            step = Steps(dve, dve_step, "dve_step")
            link, mark = step.link, step.mark

            def product(f, e):
                n = NE * f + e
                dve.wait_ge(silu_done, n + 1)
                dve.wait_ge(up_done, n + 1)
                V.tensor_tensor(act[:, e % 3], act[:, e % 3], up_ps[:, e % 2], ALU.mult).then_inc(prod_done, 1)

            def weigh(f, e):
                dve.wait_ge(prod_done, NE * f + e + 1)
                dve.wait_ge(wb_done, E * f + e)
                V.tensor_tensor(act[:, e % 3], act[:, e % 3], wb[:, e - 1], ALU.mult).then_inc(weighted, 1)

            def low(f, e):
                n = NE * f + e
                dve.wait_ge(act_hi_done, n + 1)
                if positive(n - 2):
                    dve.wait_ge(down_done, n - 2)
                V.tensor_tensor(act_lo[:, e % 3], act[:, e % 3], act_hi[:, e % 3].bitcast(F32),
                                ALU.subtract).then_inc(act_lo_done, 1)

            def core(f, e, first):
                product(f, e)
                if e >= 1:
                    low(f, e - 1)
                elif not first:
                    low(f - 1, NE - 1)
                if e >= 1:
                    weigh(f, e)

            def top(src, eq, best, value, onehot):
                link(V.tensor_reduce(best, src, AX.X, ALU.max))
                link(V.tensor_tensor(eq, src, best.unsqueeze(2).broadcast_to([P, NT, E]), ALU.is_equal))
                link(V.tensor_tensor(eq, eq, cst[:, C_RANK:C_RANK + E].unsqueeze(1).broadcast_to([P, NT, E]), ALU.mult))
                link(V.tensor_reduce(value, eq, AX.X, ALU.max))
                link(V.tensor_tensor(onehot, eq, value.unsqueeze(2).broadcast_to([P, NT, E]), ALU.is_equal))

            def stage(s, i):
                u = side_no(i, s, GROUPS) if s in SIDE else None
                if s in SIDE and s not in ("wrow1", "wrow2", "q", "k", "inv", "wo"):
                    dve.wait_ge(side_full, u + 1)
                if s in ("stat1", "statA", "stat2"):
                    src = x_next if s == "stat1" else x_mid
                    if s == "stat1":
                        dve.wait_ge(x_next_in, 16 * (i + 2))
                    for t in range(NT):
                        ins = V.bn_stats(stats[:, t], src[:, t])
                    link(ins)
                    carry_wait(dve)
                    for t in range(NT):
                        ins = V.bn_aggr(mv[:, t], stats[:, t])
                    ins.then_inc(stats_done, 1)
                elif s in NORMS:
                    src = x_next if s == "norm1" else x_mid
                    dve.wait_ge(scale_done, norm_no(i, s, GROUPS) + 1)
                    for t in range(NT):
                        ins = V.tensor_scalar(xn[:, t], src[:, t], mv[:, t, 0:1], scl[:, 7, t:t + 1],
                                              ALU.subtract, ALU.mult)
                    ins.then_inc(norm_done, 1)
                elif s in ("turn1", "turnA", "turn2"):
                    kind = s[-1]
                    for k in range(KD):
                        n = norm_no(i, "norm" + kind, GROUPS)
                        dve.wait_ge(hi_done, 2 * n + k + 1 + (0 if type(i) is int and i == -1 else 3))
                        hi = h_hi[kind][:, k].bitcast(F32)
                        if kind == "A":
                            ins = V.tensor_tensor(h_lo[kind][:, k], side[:, k], hi, ALU.subtract)
                        else:
                            ins = V.scalar_tensor_tensor(out=h_lo[kind][:, k], in0=side[:, k], scalar=rmsw[:, k:k + 1],
                                                         in1=hi, op0=ALU.mult, op1=ALU.subtract)
                    ins.then_inc(side_read, 1)
                elif s in ("route1", "route2"):
                    V.tensor_copy(lg[:, 0].rearrange("p t e -> p (t e)"), side[:, 0, 0:NT * E]
                                  ).then_inc(side_read, 1)
                    dve.wait_ge(side_read, u + 1)
                    top(lg[:, 0], lg[:, 1], rt[:, 0], rt[:, 1], lg[:, 2])
                    link(V.scalar_tensor_tensor(out=lg[:, 3].rearrange("p t e -> p (t e)"),
                                                in0=lg[:, 2].rearrange("p t e -> p (t e)"), scalar=-BIG,
                                                in1=lg[:, 0].rearrange("p t e -> p (t e)"), op0=ALU.mult, op1=ALU.add))
                    top(lg[:, 3], lg[:, 4], rt[:, 2], rt[:, 3], lg[:, 5])
                    V.tensor_tensor(rt[:, 4], rt[:, 2], rt[:, 0], ALU.subtract).then_inc(diff_done, 1)
                elif s in ("gatew1", "gatew2"):
                    dve.wait_ge(tanh_done, route_no(i, s) + 1)
                    V.tensor_scalar(rt[:, 6], rt[:, 5], -0.5, 0.5, ALU.mult, ALU.add)
                    link(V.tensor_scalar(rt[:, 7], rt[:, 5], 0.5, 0.5, ALU.mult, ALU.add))
                    V.tensor_tensor(lg[:, 1], lg[:, 2], rt[:, 6].unsqueeze(2).broadcast_to([P, NT, E]), ALU.mult)
                    link(V.tensor_tensor(lg[:, 4], lg[:, 5], rt[:, 7].unsqueeze(2).broadcast_to([P, NT, E]), ALU.mult))
                    V.tensor_tensor(wt[:].rearrange("p e t -> p t e"), lg[:, 1], lg[:, 4],
                                    ALU.add).then_inc(wt_done, 1)
                elif s == "sum1":
                    dve.wait_ge(x_in_done, i + 1)
                    if positive(i):
                        dve.wait_ge(x_last_done, i)
                    V.tensor_tensor(x_mid[:].rearrange("p t d -> p (t d)"), side[:].rearrange("p b c -> p (b c)"),
                                    x_in[:].rearrange("p t d -> p (t d)"), ALU.add).then_inc(x1_done, 1)
                    dve.wait_ge(x1_done, i + 1)
                    dve.sem_inc(side_read, 1)
                elif s == "sum2":
                    dve.wait_ge(x_last_done, i)
                    V.tensor_tensor(x_last[:].rearrange("p t d -> p (t d)"), side[:].rearrange("p b c -> p (b c)"),
                                    x_last[:].rearrange("p t d -> p (t d)"), ALU.add).then_inc(x3_done, 1)
                    dve.wait_ge(x3_done, i)
                    dve.sem_inc(side_read, 1)
                elif s == "sum3":
                    V.tensor_tensor(x_mid[:].rearrange("p t d -> p (t d)"), side[:].rearrange("p b c -> p (b c)"),
                                    x_mid[:].rearrange("p t d -> p (t d)"), ALU.add).then_inc(x2_done, 1)
                    dve.wait_ge(x2_done, i + 1)
                    dve.sem_inc(side_read, 1)
                elif s == "sq":
                    n2, y, t, rec = (nrm[:, j] for j in range(4))
                    V.tensor_copy(n2, side[:, 0, 0:P]).then_inc(side_read, 1)
                    dve.wait_ge(side_read, u + 1)
                    link(V.tensor_scalar(t.bitcast(I32), n2.bitcast(I32), 1, None, ALU.logical_shift_right))
                    link(V.tensor_scalar(y.bitcast(I32), t.bitcast(I32), -1.0, float(RSQRT_MAGIC), ALU.mult, ALU.add))
                    for _ in range(3):
                        link(V.tensor_tensor(t, y, y, ALU.mult))
                        link(V.tensor_tensor(t, t, n2, ALU.mult))
                        link(V.tensor_scalar(t, t, -0.5, 1.5, ALU.mult, ALU.add))
                        link(V.tensor_tensor(y, y, t, ALU.mult))
                    V.reciprocal(rec, n2)
                    link(V.tensor_tensor(t, y, n2, ALU.mult))
                    V.tensor_tensor(y, t, rec, ALU.mult).then_inc(inv_done, 1)
                elif s == "spread":
                    slot = (5 * i) >> 2
                    link(V.tensor_tensor(k_sb[:], k_sb[:], side[:, 1].unsqueeze(1).broadcast_to([P, 2, TOK]), ALU.mult))
                    for plane in range(2):
                        V.tensor_tensor_scan(k_sb[:, plane], one.broadcast_to([P, TOK]), k_sb[:, plane],
                                             carry[:, plane, bass.ds(slot, 1)], ALU.mult, ALU.add)
                    V.tensor_tensor(q_sb[:], q_sb[:], side[:, 0].unsqueeze(1).broadcast_to([P, 2, TOK]),
                                    ALU.mult).then_inc(side_read, 1)
                    dve.wait_ge(side_read, u + 1)
                    V.tensor_copy(carry[:, :, bass.ds(slot + 1, 1)], k_sb[:, :, TOK - 1:TOK]).then_inc(cum_done, 1)
                elif s == "conv":
                    dve.wait_ge(cum_done, i + 1)
                    V.tensor_tensor(sq_q[:], q_sb[:], k_sb[:], ALU.mult)
                    link(V.tensor_tensor(sq_k[:, 0], q_sb[:, 1], k_sb[:, 0], ALU.mult))
                    link(V.scalar_tensor_tensor(out=o_sb[:, 0], in0=sq_q[:, 1], scalar=cst[:, C_SIGN:C_SIGN + 1],
                                                in1=sq_q[:, 0], op0=ALU.mult, op1=ALU.add))
                    dve.wait_ge(cross_done, i + 1)
                    V.tensor_tensor(o_sb[:, 1], sq_k[:, 0], sq_k[:, 1], ALU.add).then_inc(o_done, 1)
                elif s == "osplit":
                    dve.wait_ge(o_hi_done, i + 1)
                    V.tensor_tensor(o_lo[:], o_sb[:], o_hi[:].bitcast(F32), ALU.subtract).then_inc(o_lo_done, 1)

            def split_expert(e):
                dve.wait_ge(w_hi_done, e + 1)
                V.tensor_tensor(w_lo[:, e], w_raw[:, e % 3], w_hi[:, e].bitcast(F32),
                                ALU.subtract).then_inc(w_lo_done, 1)

            def setup_low(name, dst, hi, scale, count):
                dve.wait_ge(hi_done, count)
                V.scalar_tensor_tensor(out=dst, in0=side[:, :, 0:D], scalar=scale, in1=hi.bitcast(F32),
                                       op0=ALU.mult, op1=ALU.subtract).then_inc(side_read, 1)

            V.memset(carry[:], 0.0)
            V.memset(scl[:, 6], -0.5).then_inc(filled, 1)
            stage("stat1", -1)
            dve.wait_ge(cst_in, 16)
            dve.wait_ge(small_in, 32)
            dve.wait_ge(router_hi_done, 1)
            V.tensor_tensor(router_lo[:], router[:], router_hi[:].bitcast(F32), ALU.subtract
                            ).then_inc(router_split, 1)
            stage("norm1", -1)
            stage("turn1", -1)
            split_expert(0)
            stage("route1", -1)
            split_expert(1)
            for e in range(NE):
                if e == 0:
                    product(0, 0)
                    stage("gatew1", -1)
                else:
                    core(0, e, True)
                if e + 2 < NE:
                    split_expert(e + 2)
                if e == 3:
                    setup_low("wq", qk_lo[:, 0], qk_hi[:, 0], 1.0, 3)
                if e == 4:
                    setup_low("wk", qk_lo[:, 1], qk_hi[:, 1], 1.0, 4)
                if e == 6:
                    setup_low("wo", wo_lo[:], wo_hi[:], CONV_SCALE, 5)
            low(0, NE - 1)

            def window(i, w):
                f = ffn_no(i, w)
                for e, (before, after) in enumerate(stages(i, STAGES_A if w == "A" else STAGES_B, GROUPS)):
                    if has_ffn(i, w):
                        core(f, e, not pending(i))
                    elif e == 0 and pending(i):
                        low(f - 1, NE - 1)
                    for s in before + after:
                        stage(s, i)

            run_periods(dve, window, (step,))
            f = 2 * GROUPS - 1
            for e in range(NE):
                core(f, e, True)
            low(f, NE - 1)
            stage("sum2", GROUPS)

        @block.gpsimd
        def _(pool):
            G = nc.gpsimd
            step = Steps(pool, pool_step, "pool_step")
            link = step.link

            def stage(s, i):
                if s in ("stat1", "statA", "stat2"):
                    n = norm_no(i, "norm" + s[-1], GROUPS)
                    var, half = mv[:, :, 1], scl[:, 6]
                    pool.wait_ge(stats_done, n + 1)
                    carry_wait(pool)
                    link(G.tensor_scalar(scl[:, 0], var, LN_EPS, None, ALU.add))
                    if s == "statA":
                        G.tensor_tensor(scl[:, 7], scl[:, 0], half, ALU.pow).then_inc(scale_done, 1)
                        return
                    link(G.tensor_tensor(scl[:, 1], scl[:, 0], half, ALU.pow))
                    link(G.tensor_tensor(scl[:, 2], scl[:, 1], scl[:, 1], ALU.mult))
                    link(G.tensor_tensor(scl[:, 3], scl[:, 2], var, ALU.mult))
                    carry_wait(pool)
                    link(G.tensor_scalar(scl[:, 4], scl[:, 3], RMS_EPS, None, ALU.add))
                    link(G.tensor_tensor(scl[:, 5], scl[:, 4], half, ALU.pow))
                    G.tensor_tensor(scl[:, 7], scl[:, 1], scl[:, 5], ALU.mult).then_inc(scale_done, 1)
                elif s in ("wspread1", "wspread2"):
                    r = route_no(i, s)
                    pool.wait_ge(wrow_in, 16 * (r + 1))
                    for e in range(E):
                        if not (type(i) is int and i == -1):
                            pool.wait_ge(weighted, E * (r - 1) + e + 1)
                        carry_wait(pool)
                        G.partition_broadcast(wb[:, e], wrow[0:1, e * TOK:(e + 1) * TOK], channels=P
                                              ).then_inc(wb_done, 1)
                elif s in ("q", "k"):
                    sq = sq_q if s == "q" else sq_k
                    pool.wait_ge(squared, 2 * i + 1 + (s == "k"))
                    G.tensor_tensor(sq[:, 0], sq[:, 0], sq[:, 1], ALU.add).then_inc(sq_summed, 1)
                elif s == "conv":
                    pool.wait_ge(cum_done, i + 1)
                    G.tensor_tensor(sq_k[:, 1], q_sb[:, 0], k_sb[:, 1], ALU.mult).then_inc(cross_done, 1)

            pool.wait_ge(filled, 1)
            stage("stat1", -1)
            stage("wspread1", -1)

            def window(i, w):
                for before, after in stages(i, STAGES_A if w == "A" else STAGES_B, GROUPS):
                    for s in before + after:
                        stage(s, i)

            run_periods(pool, window, (step,))


_INS = ["L0_attn_x", "L0_attn_W_q", "L0_attn_W_kv", "L0_attn_W_o", "L0_ffn_rms_weight", "L0_ffn_router_w",
        "L0_ffn_w_gate", "L0_ffn_w_up", "L0_ffn_w_down", "L0_ffn_sw_gate", "L0_ffn_sw_up", "L0_ffn_sw_down"]


def kernel(**inputs):
    import concourse.bacc as bacc
    from concourse.bass_utils import run_bass_kernel_spmd

    nc = bacc.Bacc("TRN2", target_bir_lowering=False, num_devices=1)
    arrays = {name: np.ascontiguousarray(inputs[name]) for name in _INS}
    arrays["constants"] = constants()
    args = [nc.dram_tensor(n, a.shape, mybir.dt.from_np(a.dtype), kind="ExternalInput").ap()
            for n, a in arrays.items()]
    args.append(nc.dram_tensor("row_dram", (E * NT, P), F32, kind="Internal").ap())
    out = nc.dram_tensor("out", arrays["L0_attn_x"].shape, F32, kind="ExternalOutput").ap()
    build(nc, *args, out)
    r = run_bass_kernel_spmd(nc, [arrays], core_ids=[0])
    return r.results[0]["out"]
```

```python
from contextlib import ExitStack

import numpy as np

import concourse.bass as bass
from concourse import mybir

ALU = mybir.AluOpType
ACT = mybir.ActivationFunctionType
AX = mybir.AxisListType
F32 = mybir.dt.float32
F32R = mybir.dt.float32r
I32 = mybir.dt.int32

P = 128
TOK = 512
NT = TOK // P
D = 256
KD = D // P
E = 8
NE = E + 1
F = 128
HEADS, HD = 16, 16
HB = HD // 2
LN_EPS, RMS_EPS = 1e-5, 1e-6
BIG = 3.0e38
RSQRT_MAGIC = 0x5F3759DF
CONV_SCALE = 1.0 / (2.0 * float(np.sqrt(HD / 2)))

WG, WU, WD, WCOLS = 0, 2 * F, 4 * F, 4 * F + D

C_ID, C_SELN, C_INDEX, C_SIGN, C_ONE, C_STAY = 0, 128, 192, 200, 201, 202
C_DFT, C_SELB = C_STAY, C_STAY + KD * D
C_COLS = C_SELB + 2 * P

STAGES_A = [
    (["wrow0", "loadx"], ["wspread0"]),
    (["stat1"], ["ycopy1"]),
    (["sum1"], ["norm1", "statA"]),
    (["turn1"], ["normA"]),
    (["turnA"], ["xa"]),
    (["q"], []),
    (["route1"], ["k", "gatew1"]),
    ([], ["sq", "wrow1", "wspread1"]),
    ([], ["sq2"]),
]
STAGES_B = [
    ([], ["inv"]),
    (["spread"], ["conv", "ycopy2"]),
    ([], ["conv2", "osplit", "sum2"]),
    ([], []),
    (["wo"], ["sum3"]),
    ([], ["stat2", "xc"]),
    ([], ["norm2"]),
    (["turn2"], []),
    (["route2"], ["gatew2"]),
]
STAGES_SETUP = [
    ([], ["loadx"]),
    (["wrow1"], []),
    ([], ["wq"]),
    ([], ["wk", "stat1"]),
    ([], ["woT", "norm1"]),
    (["wo"], ["turn1"]),
    (["route1"], []),
    (["gatew1"], []),
    (["wrow1"], ["wspread1"]),
]
STAGES_FIRST = [
    ([], []),
    ([], ["ycopy1"]),
    (["sum1"], ["statA"]),
    ([], ["normA", "xa"]),
    (["turnA"], []),
    (["q"], ["k"]),
    ([], ["sq", "sq2"]),
    (["inv"], ["spread"]),
    ([], ["conv", "conv2", "osplit"]),
    (["wo"], ["sum3", "stat2", "norm2", "turn2", "xc", "route2", "gatew2"]),
]
STAGES_LAST_A = [
    (["wrow0"], ["wspread0"]),
    ([], ["ycopy1"]),
    (["sum1"], ["statA"]),
    ([], ["normA"]),
    (["turnA"], []),
    (["q"], ["k"]),
    ([], ["sq", "sq2"]),
    (["inv"], ["spread"]),
    ([], ["conv", "conv2", "osplit"]),
    (["wo"], ["sum3", "stat2", "norm2", "turn2"]),
]
STAGES_LAST_B = [
    (["route2"], ["gatew2"]),
    (["wrow2"], ["ycopy2", "wspread2"]),
    (["sum2"], []),
    ([], []),
    ([], []),
    ([], ["xc"]),
    ([], []),
    ([], []),
    ([], []),
]
SIDE = {"turn1", "route1", "wrow0", "wrow1", "turnA", "q", "k", "sq", "inv", "spread", "wo", "sum3",
        "turn2", "route2", "wrow2", "sum1", "sum2"}
NORMS = ("norm1", "normA", "norm2")
SETUP_SIDE = ["turn1", "route1", "wrow1", "wq", "wk", "woT", "wo"]


def stages(i, window, groups):
    if type(i) is int and i == 0:
        return [] if window == "A" else STAGES_FIRST
    if type(i) is int and i == groups - 1:
        return STAGES_LAST_A if window == "A" else STAGES_LAST_B
    return STAGES_A if window == "A" else STAGES_B


def order(i, names, groups):
    first = []
    if type(i) is int and i == 0:
        first = [s for s in ("norm1", "turn1", "route1", "wrow1") if s in names]
    return first + [s for step in stages(i, "A", groups) + stages(i, "B", groups)
                    for part in step for s in part if s in names]


def period_side(i, groups):
    per, first = len(order(1, SIDE, groups)), len(SETUP_SIDE)
    if type(i) is int and i == 0:
        return first
    if type(i) is int and i == groups:
        return period_side(groups - 1, groups) + len(order(groups - 1, SIDE, groups))
    return per * i + (first + len(order(0, SIDE, groups)) - per)


def side_no(i, name, groups):
    if type(i) is int and i == -1:
        return SETUP_SIDE.index(name)
    if type(i) is int and i == groups:
        return period_side(i, groups)
    return period_side(i, groups) + order(i, SIDE, groups).index(name)


def norm_no(i, name, groups):
    if type(i) is int and i == -1:
        return 0
    return 3 * i + 1 + order(i, NORMS, groups).index(name)


def constants():
    c = np.zeros((P, C_COLS), np.float32)
    p = np.arange(P)
    c[p, C_ID + p] = 1.0
    c[p, C_SELN + p // HB] = 1.0
    c[p, C_SELN + 32 + HEADS + p // HB] = 1.0
    for m in range(P):
        for part in (0, 2 * HEADS):
            c[part + m // HB, C_SELB + m] = 1.0
            c[part + HEADS + m // HB, C_SELB + P + m] = 1.0
    c[:, C_INDEX:C_INDEX + E] = np.arange(E)
    c[:, C_SIGN] = np.where(p % HB == 0, 1.0, -1.0)
    c[:, C_ONE] = 1.0
    n = np.arange(HD)
    basis = np.zeros((2, HB, HD))
    basis[0, 0] = np.sqrt(2.0 / HD) * (n % 2 == 0)
    basis[1, 0] = np.sqrt(2.0 / HD) * (n % 2 == 1)
    for k in range(1, HB):
        basis[0, k] = np.sqrt(2.0 / HD) * np.cos(2 * np.pi * k * n / HD)
        basis[1, k] = -np.sqrt(2.0 / HD) * np.sin(2 * np.pi * k * n / HD)
    full = np.zeros((D, D), np.float32)
    for h in range(HEADS):
        for plane in range(2):
            for k in range(HB):
                full[h * HD:(h + 1) * HD, plane * P + h * HB + k] = basis[plane, k]
    c[:, C_DFT:C_SELB] = full.reshape(KD, P, D).transpose(1, 0, 2).reshape(P, KD * D)
    return c


def build(nc, x, W_q, W_kv, W_o, rms_weight, router_w, w_gate, w_up, w_down,
          sw_gate, sw_up, sw_down, consts, out):
    B, S, _ = x.shape
    GROUPS = B * S // TOK
    PER_SEQ = S // TOK
    LAST = GROUPS - 1
    assert x.shape[2] == D and PER_SEQ == 4 and S % TOK == 0

    x_rows = x.rearrange("b s d -> (b s) d")
    out_rows = out.rearrange("b s d -> (b s) d")

    with ExitStack() as ctx:
        def sb(name, shape, dt=F32):
            return ctx.enter_context(nc.sbuf_tensor(name, shape, dt))

        def sem(name):
            return ctx.enter_context(nc.semaphore(name))

        gate_ps = ctx.enter_context(nc.psum_tensor("gate_ps", [P, 2, TOK], F32))
        up_ps = ctx.enter_context(nc.psum_tensor("up_ps", [P, 2, TOK], F32))
        y_ps = ctx.enter_context(nc.psum_tensor("y_ps", [P, KD, TOK], F32))
        side = ctx.enter_context(nc.psum_tensor("side", [P, 2, TOK], F32))

        w_raw = sb("w_raw", [P, 3, WCOLS])
        w_hi = sb("w_hi", [P, NE, WCOLS], F32R)
        w_lo = sb("w_lo", [P, NE, WCOLS], F32R)
        router = sb("router", [P, KD, E])
        router_hl = sb("router_hl", [P, KD, 2 * E], F32R)
        rmsw = sb("rmsw", [P, KD])
        cst = sb("cst", [P, C_STAY])
        sel = sb("sel", [4 * HEADS, 2 * P], F32R)
        qk_hi = sb("qk_hi", [P, 2, KD, D], F32R)
        qk_lo = sb("qk_lo", [P, 2, KD, D], F32R)
        wo_hi = sb("wo_hi", [P, 2, D], F32R)
        wo_lo = sb("wo_lo", [P, 2, D], F32R)

        x_next = sb("x_next", [P, NT, D])
        x_in = sb("x_in", [P, NT, D])
        x_mid = sb("x_mid", [P, NT, D])
        x_last = sb("x_last", [P, NT, D])
        xn = sb("xn", [P, NT, D])
        stats = {k: sb(f"stats{k}", [P, NT, 6]) for k in "1A2"}
        mv = {k: sb(f"mv{k}", [P, NT, 2]) for k in "1A2"}
        scl = {k: sb(f"scl{k}", [P, 8, NT]) for k in "1A2"}
        half = sb("half", [P, NT])

        h_hi = {k: sb(f"h{k}_hi", [P, KD, TOK], F32R) for k in "1A2"}
        h_lo = {k: sb(f"h{k}_lo", [P, KD, TOK], F32R) for k in "1A2"}
        act = sb("act", [P, 3, TOK])
        act_hi = sb("act_hi", [P, 3, TOK], F32R)
        act_lo = sb("act_lo", [P, 3, TOK], F32R)
        yT = sb("yT", [P, KD, TOK])

        lg2 = sb("lg2", [P, NT, 2 * E])
        lg = sb("lg", [P, NT, E])
        top8 = sb("top8", [P, NT, E])
        top_at = sb("top_at", [P, NT, E], mybir.dt.uint32)
        onehot = sb("onehot", [P, 2, NT, E])
        share = sb("share", [P, 2, NT, E])
        rt = sb("rt", [P, 4, NT])
        wt = sb("wt", [P, E, NT])
        wT = sb("wT", [E * NT, P])
        wrow = sb("wrow", [1, E * TOK])
        wb = sb("wb", [P, E, TOK])

        q_sb = sb("q_sb", [P, 2, TOK])
        k_sb = sb("k_sb", [P, 2, TOK])
        sq_q = sb("sq_q", [P, 2, TOK])
        sq_k = sb("sq_k", [P, 2, TOK])
        nrm = sb("nrm", [P, 4, P])
        inv = sb("inv", [P, NT, 2, 2 * HEADS], F32R)
        invT = sb("invT", [4 * HEADS, TOK], F32R)
        carry = sb("carry", [P, 2, 2 * PER_SEQ + 2])
        q_root = sq_q[:, 0]
        o_sb = sq_q
        o_hi = sb("o_hi", [P, 2, TOK], F32R)
        o_lo = sb("o_lo", [P, 2, TOK], F32R)
        wq_raw, wk_raw, wo_raw, woT = q_sb, k_sb, sq_q, sq_k
        dft, sel_raw = q_sb[:, :, D:], k_sb[0:4 * HEADS, 0, D:]

        ident = cst[:, C_ID:C_ID + P]
        one = cst[:, C_ONE:C_ONE + 1]

        gate_done, up_done, down_done, silu_done = sem("gate_done"), sem("up_done"), sem("down_done"), sem("silu_done")
        prod_done, weighted, act_hi_done, act_lo_done = sem("prod_done"), sem("weighted"), sem("act_hi_done"), sem("act_lo_done")
        y_copied, side_full, side_read = sem("y_copied"), sem("side_full"), sem("side_read")
        stats_done, scale_done, norm_done, hi_done = sem("stats_done"), sem("scale_done"), sem("norm_done"), sem("hi_done")
        diff_done, tanh_done, wt_done = sem("diff_done"), sem("tanh_done"), sem("wt_done")
        wrow_in, wb_done = sem("wrow_in"), sem("wb_done")
        x_next_in, x_in_done, x1_done, x2_done = sem("x_next_in"), sem("x_in_done"), sem("x1_done"), sem("x2_done")
        x3_done, x_last_done, stored = sem("x3_done"), sem("x_last_done"), sem("stored")
        squared, sq_summed, inv_done, cum_done = sem("squared"), sem("sq_summed"), sem("inv_done"), sem("cum_done")
        q_root_done, q_scaled, k_scaled = sem("q_root_done"), sem("q_scaled"), sem("k_scaled")
        cross_done, o_done, o_hi_done, o_lo_done = sem("cross_done"), sem("o_done"), sem("o_hi_done"), sem("o_lo_done")
        w_hi_done, w_lo_done, cst_in, small_in = sem("w_hi_done"), sem("w_lo_done"), sem("cst_in"), sem("small_in")
        attn_w_in, router_hi_done, router_split, filled = sem("attn_w_in"), sem("router_hi_done"), sem("router_split"), sem("filled")
        sel_done = sem("sel_done")
        carried, dve_step, pool_step = sem("carried"), sem("dve_step"), sem("pool_step")
        raw_in = [sem(f"raw_in{r}") for r in range(3)]

        def positive(value):
            return type(value) is not int or value > 0

        def carry_wait(eng):
            eng.sem_inc(carried, 1)

        class Steps:

            def __init__(self, eng, sem, name):
                self.eng, self.sem, self.name, self.base, self.k = eng, sem, name, 0, 0

            def at(self, base):
                self.base, self.k = base, 0

            def mark(self, ins):
                ins.then_inc(self.sem, 1)
                self.k += 1
                return self.base + self.k

            def link(self, ins):
                self.eng.wait_ge(self.sem, self.mark(ins))

        def ffn_no(i, window):
            return 2 * i if window == "A" else 2 * i + 1

        def run_periods(eng, window, counted=()):
            def measured(i):
                before = [c.k for c in counted]
                window(i, "A")
                window(i, "B")
                return [c.k - b for c, b in zip(counted, before)]

            measured(0)
            starts = [c.base + c.k for c in counted]
            with eng.Fori(1, LAST) as i:
                for c, s in zip(counted, starts):
                    c.at((i - 1) * STEPS[c.name] + s)
                per = measured(i)
                assert per == [STEPS[c.name] for c in counted], per
            for c, s in zip(counted, starts):
                c.at(s + STEPS[c.name] * (LAST - 1))
            measured(LAST)

        STEPS = {"dve_step": 28, "pool_step": 6}

        def route_no(i, name):
            if type(i) is int and i == -1:
                return 0
            if name[-1] == "1":
                return 2 * i + 1
            if name[-1] == "0":
                return 2 * i
            return 2 * i + 2 - (type(i) is int and i == LAST)

        def sum_no(i, name):
            if type(i) is int and i in (0, GROUPS):
                return 0 if i == 0 else 2 * GROUPS - 1
            return 2 * i - 1 if name[-1] == "1" else 2 * i

        def h_kind(i, w):
            return "1" if w == "B" and not (type(i) is int and i == LAST) else "2"

        def turned(i, s):
            return "2" if type(i) is int and i == -1 else s[-1]

        block = ctx.enter_context(nc.Block())

        @block.sync
        def _(sp):
            def load_expert(e):
                if e >= 3:
                    sp.wait_ge(w_lo_done, e - 2)
                g, u, d = (sw_gate, sw_up, sw_down) if e == 0 else (w_gate[e - 1], w_up[e - 1], w_down[e - 1])
                r = e % 3
                sp.dma_start(w_raw[:, r, WG:WU].rearrange("p (k f) -> p k f", k=KD),
                             g.rearrange("(k p) f -> p k f", p=P)).then_inc(raw_in[r], 16)
                sp.dma_start(w_raw[:, r, WU:WD].rearrange("p (k f) -> p k f", k=KD),
                             u.rearrange("(k p) f -> p k f", p=P)).then_inc(raw_in[r], 16)
                sp.dma_start(w_raw[:, r, WD:], d).then_inc(raw_in[r], 16)

            def load_x(g):
                sp.dma_start(x_next[:], x_rows[bass.ds(g * TOK, TOK), :].rearrange("(t p) d -> p t d", p=P)
                             ).then_inc(x_next_in, 16)

            def stage(s, i):
                if s == "loadx":
                    sp.wait_ge(x_in_done, i + 1)
                    carry_wait(sp)
                    sp.wait_ge(norm_done, norm_no(i - 1, "norm1", GROUPS) + 1)
                    carry_wait(sp)
                    load_x(i + 1)
                if s in ("wrow0", "wrow1", "wrow2"):
                    sp.wait_ge(side_read, side_no(i, s, GROUPS) + 1)
                    carry_wait(sp)
                    if positive(E * route_no(i, s)):
                        sp.wait_ge(wb_done, E * route_no(i, s))
                    carry_wait(sp)
                    sp.dma_start(wrow[:, :], wT[:, :]).then_inc(wrow_in, 16)
                if s == "sum2":
                    sp.wait_ge(x3_done, i)
                    carry_wait(sp)
                    sp.dma_start(out_rows[bass.ds((i - 1) * TOK, TOK), :].rearrange("(t p) d -> p t d", p=P),
                                 x_last[:]).then_inc(stored, 16)

            load_x(0)
            sp.dma_start(cst[:], consts[:, 0:C_STAY]).then_inc(cst_in, 16)
            sp.dma_start(rmsw[:], rms_weight.rearrange("(k p) -> p k", p=P), allow_slow_non_contiguous=True).then_inc(small_in, 16)
            sp.dma_start(router[:], router_w.rearrange("(k p) e -> p k e", p=P)).then_inc(small_in, 16)
            for e in range(3):
                load_expert(e)
            for dst, src in ((wq_raw, W_q), (wk_raw, W_kv), (wo_raw, W_o)):
                sp.dma_start(dst[:, :, 0:D], src.rearrange("(k p) d -> p k d", p=P)).then_inc(attn_w_in, 16)
            sp.dma_start(dft, consts[:, C_DFT:C_SELB].rearrange("p (k d) -> p k d", k=KD)).then_inc(attn_w_in, 16)
            sp.dma_start(sel_raw, consts[0:4 * HEADS, C_SELB:]).then_inc(attn_w_in, 16)
            stage("wrow1", -1)
            stage("loadx", 0)
            for e in range(3, NE):
                load_expert(e)
            stage("wrow1", 0)

            def window(i, w):
                for before, after in stages(i, w, GROUPS):
                    for s in before + after:
                        stage(s, i)

            run_periods(sp, window)
            stage("sum2", GROUPS)
            sp.wait_ge(stored, 16 * GROUPS)

        @block.tensor
        def _(pe):
            def triple(dst, a, b, start, stop):
                (ah, al), (bh, bl) = a, b
                nc.tensor.matmul(dst, ah, bh, start=start, stop=False, skip_group_check=True)
                nc.tensor.matmul(dst, ah, bl, start=False, stop=False, skip_group_check=True)
                return nc.tensor.matmul(dst, al, bh, start=False, stop=stop, skip_group_check=True)

            def gate_up(f, e, kind):
                n = NE * f + e
                if type(f) is int and f == 0:
                    pe.wait_ge(w_hi_done, e + 1)
                    pe.wait_ge(w_lo_done, e + 1)
                last = n - (1 if e == 0 else 3 if e == 1 else 2)
                if positive(last + 1):
                    pe.wait_ge(silu_done, last + 1)
                for k in range(KD):
                    c = slice(WG + k * F, WG + (k + 1) * F)
                    ins = triple(gate_ps[:, e % 2], (w_hi[:, e, c], w_lo[:, e, c]),
                                 (h_hi[kind][:, k], h_lo[kind][:, k]), k == 0, k == KD - 1)
                ins.then_inc(gate_done, 1)
                if positive(last + 1):
                    pe.wait_ge(prod_done, last + 1)
                for k in range(KD):
                    c = slice(WU + k * F, WU + (k + 1) * F)
                    ins = triple(up_ps[:, e % 2], (w_hi[:, e, c], w_lo[:, e, c]),
                                 (h_hi[kind][:, k], h_lo[kind][:, k]), k == 0, k == KD - 1)
                ins.then_inc(up_done, 1)

            def down(f, e):
                n = NE * f + e
                pe.wait_ge(act_lo_done, n + 1)
                if e == 0:
                    if positive(f):
                        pe.wait_ge(y_copied, f)
                for m in range(KD):
                    c = slice(WD + m * P, WD + (m + 1) * P)
                    ins = triple(y_ps[:, m], (w_hi[:, e, c], w_lo[:, e, c]),
                                 (act_hi[:, e % 3], act_lo[:, e % 3]), e == 0, e == NE - 1)
                ins.then_inc(down_done, 1)

            def back(src):
                for t in range(NT):
                    for m in range(KD):
                        ins = nc.tensor.transpose(side[:, t // 2, (t % 2) * D + m * P:(t % 2) * D + (m + 1) * P],
                                                  src[:, m, t * P:(t + 1) * P], ident)
                return ins

            def stage(s, i):
                if s in SIDE:
                    u = side_no(i, s, GROUPS)
                    if s in ("turn1", "turnA", "turn2"):
                        pe.wait_ge(norm_done, norm_no(i, "norm" + s[-1], GROUPS) + 1)
                    if s in ("wrow0", "wrow1", "wrow2"):
                        pe.wait_ge(wt_done, route_no(i, s) + 1)
                    if s in ("sum1", "sum2"):
                        pe.wait_ge(y_copied, sum_no(i, s) + 1)
                    if s == "sq":
                        pe.wait_ge(sq_summed, 2 * i + 2)
                    if s == "inv":
                        pe.wait_ge(inv_done, i + 1)
                    if s == "spread" and type(i) is int and i == 0:
                        pe.wait_ge(sel_done, 1)
                    if s == "wo":
                        pe.wait_ge(o_lo_done, i + 1)
                    if positive(u):
                        pe.wait_ge(side_read, u)
                if s in ("turn1", "turnA", "turn2"):
                    for k in range(KD):
                        for t in range(NT):
                            ins = nc.tensor.transpose(side[:, k, t * P:(t + 1) * P],
                                                      xn[:, t, k * P:(k + 1) * P], ident)
                elif s in ("route1", "route2"):
                    hh, hl = h_hi[turned(i, s)], h_lo[turned(i, s)]
                    for t in range(NT):
                        for k in range(KD):
                            for part in (hh, hl):
                                ins = nc.tensor.matmul(side[:, 0, t * 2 * E:(t + 1) * 2 * E],
                                                       part[:, k, t * P:(t + 1) * P], router_hl[:, k],
                                                       start=k == 0 and part is hh, stop=k == KD - 1 and part is hl,
                                                       skip_group_check=True)
                elif s in ("wrow0", "wrow1", "wrow2"):
                    ins = nc.tensor.transpose(side[0:E * NT, 1, 0:P], wt[:].rearrange("p e t -> p (e t)"), ident)
                elif s in ("sum1", "sum2", "sum3"):
                    ins = back(yT)
                elif s in ("q", "k"):
                    j = "qk".index(s)
                    for plane in range(2):
                        for k in range(KD):
                            c = slice(plane * P, (plane + 1) * P)
                            ins = triple(side[:, plane], (qk_hi[:, j, k, c], qk_lo[:, j, k, c]),
                                         (h_hi["A"][:, k], h_lo["A"][:, k]), k == 0, k == KD - 1)
                elif s == "sq":
                    for t in range(NT):
                        dst = side[:, 0, 2 * HEADS * t:2 * HEADS * (t + 1)]
                        c = slice(t * P, (t + 1) * P)
                        nc.tensor.matmul(dst, sq_q[:, 0, c], cst[:, C_SELN:C_SELN + 32],
                                         start=True, stop=False, skip_group_check=True)
                        ins = nc.tensor.matmul(dst, sq_k[:, 0, c], cst[:, C_SELN + 32:C_SELN + 64],
                                               start=False, stop=True, skip_group_check=True)
                elif s == "inv":
                    carry_wait(pe)
                    for t in range(NT):
                        ins = nc.tensor.transpose(side[0:4 * HEADS, 1, t * P:(t + 1) * P],
                                                  inv[:, t].rearrange("p a b -> p (a b)").bitcast(F32), ident)
                elif s == "spread":
                    for j in range(2):
                        ins = nc.tensor.matmul(side[:, j], sel[:, j * P:(j + 1) * P], invT[:], start=True, stop=True)
                elif s == "wo":
                    for m in range(KD):
                        for plane in range(2):
                            c = slice(m * P, (m + 1) * P)
                            ins = triple(side[:, m], (wo_hi[:, plane, c], wo_lo[:, plane, c]),
                                         (o_hi[:, plane], o_lo[:, plane]), plane == 0, plane == 1)
                else:
                    return
                ins.then_inc(side_full, 1)

            def fold(name, raw):
                pe.wait_ge(side_read, SETUP_SIDE.index(name))
                pe.wait_ge(attn_w_in, 80)
                for m in range(KD):
                    for k in range(KD):
                        ins = nc.tensor.matmul(side[:, m, 0:D], raw[:, k, m * P:(m + 1) * P],
                                               dft[:, k],
                                               start=k == 0, stop=k == KD - 1)
                ins.then_inc(side_full, 1)

            def turn_wo():
                pe.wait_ge(side_read, SETUP_SIDE.index("woT"))
                for m in range(KD):
                    for k in range(KD):
                        ins = nc.tensor.transpose(side[:, m, k * P:(k + 1) * P],
                                                  wo_raw[:, k, m * P:(m + 1) * P], ident)
                ins.then_inc(side_full, 1)

            def fold_wo():
                pe.wait_ge(side_read, SETUP_SIDE.index("wo"))
                for plane in range(2):
                    for k in range(KD):
                        ins = nc.tensor.matmul(side[:, plane, 0:D], dft[:, k, plane * P:(plane + 1) * P], woT[:, k, 0:D],
                                               start=k == 0, stop=k == KD - 1)
                ins.then_inc(side_full, 1)

            pe.wait_ge(cst_in, 16)
            stage("turn1", -1)
            pe.wait_ge(router_split, 1)
            stage("route1", -1)
            for e in range(NE):
                before, after = STAGES_SETUP[e]
                gate_up(0, e, "2")
                for s in before:
                    if s == "wo":
                        fold_wo()
                    else:
                        stage(s, -1 if e == 1 else 0)
                if e >= 2:
                    down(0, e - 2)
                for s in after:
                    if s == "wq":
                        fold("wq", wq_raw)
                    elif s == "wk":
                        fold("wk", wk_raw)
                    elif s == "woT":
                        turn_wo()
                    else:
                        stage(s, 0)

            def window(i, w):
                f = ffn_no(i, w)
                for e, (before, after) in enumerate(stages(i, w, GROUPS)):
                    if type(i) is int and i == LAST and w == "B" and e == 0:
                        pe.wait_ge(side_read, side_no(i, "turn2", GROUPS) + 1)
                    if e < NE:
                        gate_up(f, e, h_kind(i, w))
                    for s in before:
                        stage(s, i)
                    if e < 2:
                        down(f - 1, NE - 2 + e)
                    elif e < NE:
                        down(f, e - 2)
                    for s in after:
                        stage(s, i)

            run_periods(pe, window)
            down(2 * GROUPS - 1, NE - 2)
            down(2 * GROUPS - 1, NE - 1)
            stage("sum2", GROUPS)

        @block.scalar
        def _(act_e):
            A = nc.scalar

            def silu(f, e):
                n = NE * f + e
                act_e.wait_ge(gate_done, n + 1)
                if positive(n - 2):
                    act_e.wait_ge(act_lo_done, n - 2)
                A.activation(act[:, e % 3], gate_ps[:, e % 2], ACT.Silu).then_inc(silu_done, 1)

            def high(f, e):
                n = NE * f + e
                if e == 0:
                    act_e.wait_ge(prod_done, n + 1)
                else:
                    act_e.wait_ge(weighted, E * f + e)
                if positive(n - 2):
                    act_e.wait_ge(down_done, n - 2)
                A.activation(act_hi[:, e % 3], act[:, e % 3], ACT.Copy).then_inc(act_hi_done, 1)

            def core(f, e):
                silu(f, e)
                if e >= 1:
                    high(f, e - 1)
                elif positive(f):
                    high(f - 1, NE - 1)

            def stage(s, i):
                full = side_no(i, s, GROUPS) + 1 if s in SIDE else None
                if s in NORMS:
                    src, kind = (x_next if s == "norm1" else x_mid), s[-1]
                    act_e.wait_ge(scale_done, norm_no(i, s, GROUPS) + 1)
                    for t in range(NT):
                        ins = A.activation(xn[:, t], src[:, t], ACT.Identity, bias=scl[kind][:, 6, t:t + 1],
                                           scale=scl[kind][:, 7, t:t + 1])
                    ins.then_inc(norm_done, 1)
                elif s in ("turn1", "turnA", "turn2"):
                    kind = turned(i, s)
                    act_e.wait_ge(side_full, full)
                    for k in range(KD):
                        if kind == "A":
                            ins = A.activation(h_hi[kind][:, k], side[:, k], ACT.Copy)
                        else:
                            ins = A.activation(h_hi[kind][:, k], side[:, k], ACT.Copy, scale=rmsw[:, k:k + 1])
                        ins.then_inc(hi_done, 1)
                elif s in ("gatew1", "gatew2"):
                    act_e.wait_ge(diff_done, route_no(i, s) + 1)
                    A.activation(rt[:, 1], rt[:, 0], ACT.Tanh, scale=0.5).then_inc(tanh_done, 1)
                elif s in ("wrow0", "wrow1", "wrow2"):
                    act_e.wait_ge(side_full, full)
                    if positive(16 * route_no(i, s)):
                        act_e.wait_ge(wrow_in, 16 * route_no(i, s))
                    A.copy(wT[:, :], side[0:E * NT, 1, 0:P]).then_inc(side_read, 1)
                elif s in ("ycopy1", "ycopy2"):
                    act_e.wait_ge(down_done, NE * (sum_no(i, s) + 1))
                    if s == "ycopy1":
                        act_e.wait_ge(side_read, period_side(i, GROUPS))
                    elif type(i) is int and i == LAST:
                        act_e.wait_ge(x2_done, GROUPS)
                    elif type(i) is int and i == GROUPS:
                        act_e.wait_ge(x3_done, LAST)
                    else:
                        act_e.wait_ge(x1_done, i + 1)
                    A.activation(yT[:], y_ps[:], ACT.Copy, scale=0.5).then_inc(y_copied, 1)
                elif s == "xa":
                    act_e.wait_ge(x1_done, i + 1)
                    act_e.wait_ge(x_next_in, 16 * (i + 2))
                    A.copy(x_in[:], x_next[:]).then_inc(x_in_done, 1)
                elif s == "xc":
                    act_e.wait_ge(x2_done, i + 1)
                    if positive(16 * i):
                        act_e.wait_ge(stored, 16 * i)
                    A.copy(x_last[:], x_mid[:]).then_inc(x_last_done, 1)
                elif s in ("q", "k"):
                    act_e.wait_ge(side_full, full)
                    sq, dst = (sq_q, q_sb) if s == "q" else (sq_k, k_sb)
                    A.activation(sq[:], side[:], ACT.Square).then_inc(squared, 1)
                    A.copy(dst[:], side[:]).then_inc(side_read, 1)
                elif s == "inv":
                    act_e.wait_ge(side_full, full)
                    A.copy(invT[:, :], side[0:4 * HEADS, 1, :]).then_inc(side_read, 1)
                elif s == "spread":
                    act_e.wait_ge(side_full, full)
                    A.copy(q_root, side[:, 0]).then_inc(q_root_done, 1)
                elif s == "osplit":
                    for plane in range(2):
                        act_e.wait_ge(o_done, 2 * i + 1 + plane)
                        A.activation(o_hi[:, plane], o_sb[:, plane], ACT.Copy).then_inc(o_hi_done, 1)
                elif s == "wo":
                    act_e.wait_ge(side_full, full)
                    A.copy(yT[:], side[:]).then_inc(side_read, 1)

            def split_expert(e):
                act_e.wait_ge(raw_in[e % 3], 48 * (e // 3 + 1))
                A.activation(w_hi[:, e], w_raw[:, e % 3], ACT.Copy).then_inc(w_hi_done, 1)

            def setup_high(name, dst, scale):
                act_e.wait_ge(side_full, SETUP_SIDE.index(name) + 1)
                A.activation(dst, side[:, :, 0:D], ACT.Copy, scale=scale).then_inc(hi_done, 1)

            act_e.wait_ge(small_in, 32)
            A.activation(router_hl[:, :, 0:E], router[:], ACT.Copy).then_inc(router_hi_done, 1)
            split_expert(0)
            act_e.wait_ge(x_next_in, 16)
            stage("norm1", -1)
            A.copy(x_in[:], x_next[:]).then_inc(x_in_done, 1)
            stage("turn1", -1)
            split_expert(1)
            for e in range(NE):
                core(0, e)
                if e == 0:
                    stage("gatew1", -1)
                if e == 1:
                    stage("wrow1", -1)
                if e + 2 < NE:
                    split_expert(e + 2)
                before, after = STAGES_SETUP[e]
                for s in before + after:
                    if s == "wq":
                        setup_high("wq", qk_hi[:, 0], 1.0)
                    elif s == "wk":
                        setup_high("wk", qk_hi[:, 1], 1.0)
                    elif s == "woT":
                        act_e.wait_ge(side_full, SETUP_SIDE.index("woT") + 1)
                        A.copy(woT[:, :, 0:D], side[:, :, 0:D]).then_inc(side_read, 1)
                        A.copy(sel[:, :], sel_raw).then_inc(sel_done, 1)
                    elif s == "wo":
                        setup_high("wo", wo_hi[:], CONV_SCALE)
                    elif s == "loadx" or e > 1:
                        stage(s, 0)

            def window(i, w):
                f = ffn_no(i, w)
                for e, (before, after) in enumerate(stages(i, w, GROUPS)):
                    if e < NE:
                        core(f, e)
                    for s in before + after:
                        stage(s, i)

            run_periods(act_e, window)
            high(2 * GROUPS - 1, NE - 1)
            stage("ycopy2", GROUPS)

        @block.vector
        def _(dve):
            V = nc.vector
            step = Steps(dve, dve_step, "dve_step")
            link, mark = step.link, step.mark

            def product(f, e):
                n = NE * f + e
                dve.wait_ge(silu_done, n + 1)
                dve.wait_ge(up_done, n + 1)
                V.tensor_tensor(act[:, e % 3], act[:, e % 3], up_ps[:, e % 2], ALU.mult).then_inc(prod_done, 1)

            def weigh(f, e):
                dve.wait_ge(prod_done, NE * f + e + 1)
                dve.wait_ge(wb_done, E * f + e)
                V.tensor_tensor(act[:, e % 3], act[:, e % 3], wb[:, e - 1], ALU.mult).then_inc(weighted, 1)

            def low(f, e):
                n = NE * f + e
                dve.wait_ge(act_hi_done, n + 1)
                if positive(n - 2):
                    dve.wait_ge(down_done, n - 2)
                V.tensor_tensor(act_lo[:, e % 3], act[:, e % 3], act_hi[:, e % 3].bitcast(F32),
                                ALU.subtract).then_inc(act_lo_done, 1)

            def core(f, e):
                product(f, e)
                if e >= 1:
                    low(f, e - 1)
                elif positive(f):
                    low(f - 1, NE - 1)
                if e >= 1:
                    weigh(f, e)

            def newton():
                n2, y, t = (nrm[:, j] for j in range(3))
                link(V.tensor_tensor(t, y, y, ALU.mult))
                link(V.scalar_tensor_tensor(out=t, in0=t, scalar=-0.5, in1=n2, op0=ALU.mult, op1=ALU.mult))
                link(V.scalar_tensor_tensor(out=y, in0=t, scalar=1.5, in1=y, op0=ALU.add, op1=ALU.mult))

            def stage(s, i):
                u = side_no(i, s, GROUPS) if s in SIDE else None
                if s in SIDE and s not in ("wrow0", "wrow1", "wrow2", "q", "k", "inv", "wo"):
                    dve.wait_ge(side_full, u + 1)
                if s in ("stat1", "statA", "stat2"):
                    src = x_next if s == "stat1" else x_mid
                    if s == "stat1":
                        dve.wait_ge(x_next_in, 16 * (i + 2))
                    for t in range(NT):
                        ins = V.bn_stats(stats[s[-1]][:, t], src[:, t])
                    link(ins)
                    carry_wait(dve)
                    for t in range(NT):
                        ins = V.bn_aggr(mv[s[-1]][:, t], stats[s[-1]][:, t])
                    ins.then_inc(stats_done, 1)
                elif s in ("turn1", "turnA", "turn2"):
                    kind = turned(i, s)
                    for k in range(KD):
                        n = norm_no(i, "norm" + s[-1], GROUPS)
                        dve.wait_ge(hi_done, 2 * n + k + 1 + (0 if type(i) is int and i == -1 else 3))
                        hi = h_hi[kind][:, k].bitcast(F32)
                        if kind == "A":
                            ins = V.tensor_tensor(h_lo[kind][:, k], side[:, k], hi, ALU.subtract)
                        else:
                            ins = V.scalar_tensor_tensor(out=h_lo[kind][:, k], in0=side[:, k], scalar=rmsw[:, k:k + 1],
                                                         in1=hi, op0=ALU.mult, op1=ALU.subtract)
                    ins.then_inc(side_read, 1)
                elif s in ("route1", "route2"):
                    V.tensor_copy(lg2[:].rearrange("p t e -> p (t e)"), side[:, 0, 0:NT * 2 * E]).then_inc(side_read, 1)
                    dve.wait_ge(side_read, u + 1)
                    link(V.tensor_tensor(lg[:], lg2[:, :, 0:E], lg2[:, :, E:], ALU.add))
                    carry_wait(dve)
                    for t in range(NT):
                        ins = V.max(top8[:, t], lg[:, t])
                    link(ins)
                    carry_wait(dve)
                    for t in range(NT):
                        ins = V.max_index(top_at[:, t], top8[:, t], lg[:, t])
                    link(ins)
                    for j in range(2):
                        V.tensor_tensor(onehot[:, j], cst[:, C_INDEX:C_INDEX + E].unsqueeze(1).broadcast_to([P, NT, E]),
                                        top_at[:, :, j:j + 1].broadcast_to([P, NT, E]), ALU.is_equal)
                    V.tensor_tensor(rt[:, 0], top8[:, :, 1], top8[:, :, 0], ALU.subtract).then_inc(diff_done, 1)
                elif s in ("gatew1", "gatew2"):
                    dve.wait_ge(tanh_done, route_no(i, s) + 1)
                    V.tensor_scalar(rt[:, 2], rt[:, 1], -0.5, 0.5, ALU.mult, ALU.add)
                    link(V.tensor_scalar(rt[:, 3], rt[:, 1], 0.5, 0.5, ALU.mult, ALU.add))
                    link(V.tensor_tensor(share[:], onehot[:], rt[:, 2:4].unsqueeze(3).broadcast_to([P, 2, NT, E]),
                                         ALU.mult))
                    V.tensor_tensor(wt[:].rearrange("p e t -> p t e"), share[:, 0], share[:, 1],
                                    ALU.add).then_inc(wt_done, 1)
                elif s == "sum1":
                    dve.wait_ge(x_in_done, i + 1)
                    if positive(i):
                        dve.wait_ge(x_last_done, i)
                    V.tensor_tensor(x_mid[:].rearrange("p t d -> p (t d)"), side[:].rearrange("p b c -> p (b c)"),
                                    x_in[:].rearrange("p t d -> p (t d)"), ALU.add).then_inc(x1_done, 1)
                    dve.wait_ge(x1_done, i + 1)
                    dve.sem_inc(side_read, 1)
                elif s == "sum2":
                    dve.wait_ge(x_last_done, i)
                    V.tensor_tensor(x_last[:].rearrange("p t d -> p (t d)"), side[:].rearrange("p b c -> p (b c)"),
                                    x_last[:].rearrange("p t d -> p (t d)"), ALU.add).then_inc(x3_done, 1)
                    dve.wait_ge(x3_done, i)
                    dve.sem_inc(side_read, 1)
                elif s == "sum3":
                    V.tensor_tensor(x_mid[:].rearrange("p t d -> p (t d)"), side[:].rearrange("p b c -> p (b c)"),
                                    x_mid[:].rearrange("p t d -> p (t d)"), ALU.add).then_inc(x2_done, 1)
                    dve.wait_ge(x2_done, i + 1)
                    dve.sem_inc(side_read, 1)
                elif s == "sq":
                    n2, y, t, zero = (nrm[:, j] for j in range(4))
                    V.tensor_copy(n2, side[:, 0, 0:P]).then_inc(side_read, 1)
                    dve.wait_ge(side_read, u + 1)
                    link(V.tensor_scalar(t.bitcast(I32), n2.bitcast(I32), 1, None, ALU.logical_shift_right))
                    link(V.tensor_scalar(y.bitcast(I32), t.bitcast(I32), -1.0, float(RSQRT_MAGIC), ALU.mult, ALU.add))
                    V.tensor_scalar(zero, n2, 0.0, BIG, ALU.is_equal, ALU.mult)
                    newton()
                elif s == "sq2":
                    newton()
                    newton()
                    link(V.scalar_tensor_tensor(out=nrm[:, 1], in0=nrm[:, 3], scalar=BIG, in1=nrm[:, 1],
                                                op0=ALU.mult, op1=ALU.add))
                    root = nrm[:, 1].rearrange("p (t h) -> p t h", t=NT)
                    link(V.tensor_copy(inv[:, :, 0], root))
                    V.tensor_tensor(inv[:, :, 1], root, inv[:, :, 0].bitcast(F32), ALU.subtract).then_inc(inv_done, 1)
                elif s == "spread":
                    slot = (5 * i) >> 2
                    V.tensor_tensor(k_sb[:], k_sb[:], side[:, 1].unsqueeze(1).broadcast_to([P, 2, TOK]),
                                    ALU.mult).then_inc(k_scaled, 1)
                    dve.wait_ge(q_root_done, i + 1)
                    dve.wait_ge(k_scaled, i + 1)
                    dve.sem_inc(side_read, 1)
                    for plane in range(2):
                        ins = V.tensor_tensor_scan(k_sb[:, plane], one.broadcast_to([P, TOK]), k_sb[:, plane],
                                                   carry[:, plane, bass.ds(slot, 1)], ALU.mult, ALU.add)
                    link(ins)
                    V.tensor_copy(carry[:, :, bass.ds(slot + 1, 1)], k_sb[:, :, TOK - 1:TOK]).then_inc(cum_done, 1)
                elif s == "conv":
                    dve.wait_ge(q_scaled, i + 1)
                    V.tensor_tensor(sq_q[:], q_sb[:], k_sb[:], ALU.mult)
                    link(V.tensor_tensor(sq_k[:, 0], q_sb[:, 1], k_sb[:, 0], ALU.mult))
                elif s == "conv2":
                    V.scalar_tensor_tensor(out=o_sb[:, 0], in0=sq_q[:, 1], scalar=cst[:, C_SIGN:C_SIGN + 1],
                                           in1=sq_q[:, 0], op0=ALU.mult, op1=ALU.add).then_inc(o_done, 1)
                    dve.wait_ge(o_done, 2 * i + 1)
                    dve.wait_ge(cross_done, i + 1)
                    V.tensor_tensor(o_sb[:, 1], sq_k[:, 0], sq_k[:, 1], ALU.add).then_inc(o_done, 1)
                elif s == "osplit":
                    for plane in range(2):
                        dve.wait_ge(o_hi_done, 2 * i + 1 + plane)
                        ins = V.tensor_tensor(o_lo[:, plane], o_sb[:, plane], o_hi[:, plane].bitcast(F32), ALU.subtract)
                    ins.then_inc(o_lo_done, 1)

            def split_expert(e):
                dve.wait_ge(w_hi_done, e + 1)
                V.tensor_tensor(w_lo[:, e], w_raw[:, e % 3], w_hi[:, e].bitcast(F32),
                                ALU.subtract).then_inc(w_lo_done, 1)

            def setup_low(name, dst, hi, scale, count):
                dve.wait_ge(hi_done, count)
                V.scalar_tensor_tensor(out=dst, in0=side[:, :, 0:D], scalar=scale, in1=hi.bitcast(F32),
                                       op0=ALU.mult, op1=ALU.subtract).then_inc(side_read, 1)

            V.memset(carry[:], 0.0)
            V.memset(half[:], -0.5).then_inc(filled, 1)
            stage("stat1", -1)
            dve.wait_ge(cst_in, 16)
            dve.wait_ge(small_in, 32)
            dve.wait_ge(router_hi_done, 1)
            V.tensor_tensor(router_hl[:, :, E:], router[:], router_hl[:, :, 0:E].bitcast(F32), ALU.subtract
                            ).then_inc(router_split, 1)
            split_expert(0)
            stage("turn1", -1)
            stage("route1", -1)
            split_expert(1)
            for e in range(NE):
                if e == 1:
                    stage("gatew1", -1)
                core(0, e)
                if e + 2 < NE:
                    split_expert(e + 2)
                before, after = STAGES_SETUP[e]
                for s in before + after:
                    if s == "wq":
                        setup_low("wq", qk_lo[:, 0], qk_hi[:, 0], 1.0, 3)
                    elif s == "wk":
                        setup_low("wk", qk_lo[:, 1], qk_hi[:, 1], 1.0, 4)
                    elif s == "wo":
                        setup_low("wo", wo_lo[:], wo_hi[:], CONV_SCALE, 5)
                    elif s == "loadx" or e > 1:
                        stage(s, 0)

            def window(i, w):
                f = ffn_no(i, w)
                for e, (before, after) in enumerate(stages(i, w, GROUPS)):
                    if e < NE:
                        core(f, e)
                    for s in before + after:
                        stage(s, i)

            run_periods(dve, window, (step,))
            low(2 * GROUPS - 1, NE - 1)
            stage("sum2", GROUPS)

        @block.gpsimd
        def _(pool):
            G = nc.gpsimd
            step = Steps(pool, pool_step, "pool_step")
            link = step.link

            def stage(s, i):
                if s in ("stat1", "statA", "stat2"):
                    n = norm_no(i, "norm" + s[-1], GROUPS)
                    mean, var, scl_k = mv[s[-1]][:, :, 0], mv[s[-1]][:, :, 1], scl[s[-1]]
                    pool.wait_ge(stats_done, n + 1)
                    carry_wait(pool)
                    if s == "statA":
                        link(G.tensor_scalar(scl_k[:, 0], var, LN_EPS, None, ALU.add))
                    else:
                        link(G.tensor_scalar(scl_k[:, 0], var, 1.0 + RMS_EPS, LN_EPS * RMS_EPS, ALU.mult, ALU.add))
                    G.tensor_tensor(scl_k[:, 7], scl_k[:, 0], half[:], ALU.pow)
                    link(G.tensor_scalar(scl_k[:, 5], mean, -1.0, None, ALU.mult))
                    G.tensor_tensor(scl_k[:, 6], scl_k[:, 5], scl_k[:, 7], ALU.mult).then_inc(scale_done, 1)
                elif s in ("wspread0", "wspread1", "wspread2"):
                    r = route_no(i, s)
                    pool.wait_ge(wrow_in, 16 * (r + 1))
                    for e in range(E):
                        if not (type(i) is int and i == -1):
                            pool.wait_ge(weighted, E * (r - 1) + e + 1)
                        carry_wait(pool)
                        G.partition_broadcast(wb[:, e], wrow[0:1, e * TOK:(e + 1) * TOK], channels=P
                                              ).then_inc(wb_done, 1)
                elif s in ("q", "k"):
                    sq = sq_q if s == "q" else sq_k
                    pool.wait_ge(squared, 2 * i + 1 + (s == "k"))
                    G.tensor_tensor(sq[:, 0], sq[:, 0], sq[:, 1], ALU.add).then_inc(sq_summed, 1)
                elif s == "spread":
                    pool.wait_ge(q_root_done, i + 1)
                    G.tensor_tensor(q_sb[:], q_sb[:], q_root.unsqueeze(1).broadcast_to([P, 2, TOK]),
                                    ALU.mult).then_inc(q_scaled, 1)
                elif s == "conv":
                    pool.wait_ge(cum_done, i + 1)
                    pool.wait_ge(q_scaled, i + 1)
                    G.tensor_tensor(sq_k[:, 1], q_sb[:, 0], k_sb[:, 1], ALU.mult).then_inc(cross_done, 1)

            pool.wait_ge(filled, 1)
            stage("stat1", -1)
            stage("wspread1", -1)
            stage("stat1", 0)
            stage("wspread1", 0)

            def window(i, w):
                for before, after in stages(i, w, GROUPS):
                    for s in before + after:
                        stage(s, i)

            run_periods(pool, window, (step,))


_INS = ["L0_attn_x", "L0_attn_W_q", "L0_attn_W_kv", "L0_attn_W_o", "L0_ffn_rms_weight", "L0_ffn_router_w",
        "L0_ffn_w_gate", "L0_ffn_w_up", "L0_ffn_w_down", "L0_ffn_sw_gate", "L0_ffn_sw_up", "L0_ffn_sw_down"]


def kernel(**inputs):
    import concourse.bacc as bacc
    from concourse.bass_utils import run_bass_kernel_spmd

    nc = bacc.Bacc("TRN2", target_bir_lowering=False, num_devices=1)
    arrays = {name: np.ascontiguousarray(inputs[name]) for name in _INS}
    arrays["constants"] = constants()
    args = [nc.dram_tensor(n, a.shape, mybir.dt.from_np(a.dtype), kind="ExternalInput").ap()
            for n, a in arrays.items()]
    out = nc.dram_tensor("out", arrays["L0_attn_x"].shape, F32, kind="ExternalOutput").ap()
    build(nc, *args, out)
    r = run_bass_kernel_spmd(nc, [arrays], core_ids=[0])
    return r.results[0]["out"]
```

```python
from contextlib import ExitStack

import numpy as np

import concourse.bass as bass
from concourse import mybir

ALU = mybir.AluOpType
ACT = mybir.ActivationFunctionType
F32 = mybir.dt.float32
F32R = mybir.dt.float32r
I32 = mybir.dt.int32

P = 128
TOK = 512
NT = TOK // P
D = 256
KD = D // P
E = 8
NE = E + 1
F = 128
HEADS, HD = 16, 16
HB = HD // 2
LN_EPS, RMS_EPS = 1e-5, 1e-6
BIG = 3.0e38
RSQRT_MAGIC = 0x5F3759DF
CONV_SCALE = 1.0 / (2.0 * float(np.sqrt(HD / 2)))

WG, WU, WD, WCOLS = 0, 2 * F, 4 * F, 4 * F + D

C_ID, C_SELN, C_INDEX, C_SIGN, C_ONE, C_STAY = 0, 128, 192, 200, 201, 202
C_DFT, C_SELB = C_STAY, C_STAY + KD * D
C_COLS = C_SELB + 2 * P

STAGES_A = [
    (["loadx", "wrow0"], ["wspread0"]),
    ([], ["sum1", "statA"]),
    ([], ["normA", "stat1"]),
    ([], ["turnA"]),
    (["norm1"], ["q", "xa"]),
    (["k"], []),
    (["sq"], ["turn1"]),
    (["route1"], ["gatew1", "sq2"]),
    (["wrow1"], ["wspread1"]),
]
STAGES_B = [
    (["inv"], ["spread"]),
    ([], ["sum2", "conv"]),
    ([], ["conv2", "osplit"]),
    ([], []),
    (["wo"], ["stat2"]),
    ([], ["xc", "norm2"]),
    ([], ["turn2"]),
    (["route2"], ["gatew2"]),
    ([], []),
]
STAGES_SETUP = [
    ([], ["loadx"]),
    (["wrow1"], []),
    ([], ["wq"]),
    ([], ["wk", "stat1"]),
    ([], ["woT", "norm1"]),
    (["wo"], ["turn1"]),
    (["route1"], []),
    (["gatew1"], []),
    (["wrow1"], ["wspread1"]),
]
STAGES_FIRST = [
    ([], []),
    ([], ["sum1", "statA"]),
    (["normA"], []),
    ([], ["turnA"]),
    (["q"], ["k"]),
    (["sq", "sq2"], ["xa"]),
    ([], ["inv", "spread", "conv", "conv2", "osplit"]),
    ([], []),
    (["wo"], ["warm_norm", "stat2", "norm2", "turn2", "warm_split", "xc", "route2", "gatew2"]),
]
STAGES_LAST_A = [
    (["wrow0"], ["wspread0"]),
    ([], ["sum1", "statA"]),
    (["normA"], []),
    ([], ["turnA"]),
    (["q"], ["k"]),
    (["sq", "sq2"], []),
    ([], ["inv", "spread", "conv", "conv2", "osplit"]),
    ([], []),
    (["wo"], ["end7", "warm_end", "stat2", "end8", "norm2", "turn2", "warm_split", "route2", "gatew2"]),
]
STAGES_LAST_B = [
    (["wrow2"], ["sum2", "wspread2"]),
    ([], []),
    ([], []),
    ([], []),
    ([], []),
    ([], ["xc"]),
    ([], []),
    ([], []),
    ([], []),
]
SIDE = {"turn1", "route1", "wrow0", "wrow1", "turnA", "q", "k", "sq", "inv", "spread", "wo",
        "turn2", "route2", "wrow2"}
WARM = {"warm_start": 22, "warm_norm": 44, "warm_end": 20, "warm_split": 22}
NORMS = ("norm1", "normA", "norm2")
SETUP_SIDE = ["turn1", "route1", "wrow1", "wq", "wk", "woT", "wo"]


def stages(i, window, groups):
    if type(i) is int and i == 0:
        return [] if window == "A" else STAGES_FIRST
    if type(i) is int and i == groups - 1:
        return STAGES_LAST_A if window == "A" else STAGES_LAST_B
    return STAGES_A if window == "A" else STAGES_B


def order(i, names, groups):
    first = []
    if type(i) is int and i == 0:
        first = [s for s in ("norm1", "turn1", "route1", "wrow1") if s in names]
    return first + [s for step in stages(i, "A", groups) + stages(i, "B", groups)
                    for part in step for s in part if s in names]


def period_side(i, groups):
    per, first = len(order(1, SIDE, groups)), len(SETUP_SIDE)
    if type(i) is int and i == 0:
        return first
    if type(i) is int and i == groups:
        return period_side(groups - 1, groups) + len(order(groups - 1, SIDE, groups))
    return per * i + (first + len(order(0, SIDE, groups)) - per)


def side_no(i, name, groups):
    if type(i) is int and i == -1:
        return SETUP_SIDE.index(name)
    if type(i) is int and i == groups:
        return period_side(i, groups)
    return period_side(i, groups) + order(i, SIDE, groups).index(name)


def norm_no(i, name, groups):
    if type(i) is int and i == -1:
        return 0
    return 3 * i + 1 + order(i, NORMS, groups).index(name)


def constants():
    c = np.zeros((P, C_COLS), np.float32)
    p = np.arange(P)
    c[p, C_ID + p] = 1.0
    c[p, C_SELN + p // HB] = 1.0
    c[p, C_SELN + 32 + HEADS + p // HB] = 1.0
    for m in range(P):
        for part in (0, 2 * HEADS):
            c[part + m // HB, C_SELB + m] = 1.0
            c[part + HEADS + m // HB, C_SELB + P + m] = 1.0
    c[:, C_INDEX:C_INDEX + E] = np.arange(E)
    c[:, C_SIGN] = np.where(p % HB == 0, 1.0, -1.0)
    c[:, C_ONE] = 1.0
    n = np.arange(HD)
    basis = np.zeros((2, HB, HD))
    basis[0, 0] = np.sqrt(2.0 / HD) * (n % 2 == 0)
    basis[1, 0] = np.sqrt(2.0 / HD) * (n % 2 == 1)
    for k in range(1, HB):
        basis[0, k] = np.sqrt(2.0 / HD) * np.cos(2 * np.pi * k * n / HD)
        basis[1, k] = -np.sqrt(2.0 / HD) * np.sin(2 * np.pi * k * n / HD)
    full = np.zeros((D, D), np.float32)
    for h in range(HEADS):
        for plane in range(2):
            for k in range(HB):
                full[h * HD:(h + 1) * HD, plane * P + h * HB + k] = basis[plane, k]
    c[:, C_DFT:C_SELB] = full.reshape(KD, P, D).transpose(1, 0, 2).reshape(P, KD * D)
    return c


def build(nc, x, W_q, W_kv, W_o, rms_weight, router_w, w_gate, w_up, w_down,
          sw_gate, sw_up, sw_down, consts, out):
    B, S, _ = x.shape
    GROUPS = B * S // TOK
    PER_SEQ = S // TOK
    LAST = GROUPS - 1
    assert x.shape[2] == D and PER_SEQ == 4 and S % TOK == 0

    x_rows = x.rearrange("b s d -> (b s) d")
    out_rows = out.rearrange("b s d -> (b s) d")

    with ExitStack() as ctx:
        def sb(name, shape, dt=F32):
            return ctx.enter_context(nc.sbuf_tensor(name, shape, dt))

        def sem(name):
            return ctx.enter_context(nc.semaphore(name))

        gate_ps = ctx.enter_context(nc.psum_tensor("gate_ps", [P, 2, TOK], F32))
        up_ps = ctx.enter_context(nc.psum_tensor("up_ps", [P, 2, TOK], F32))
        y_ps = ctx.enter_context(nc.psum_tensor("y_ps", [P, NT, D], F32))
        side = ctx.enter_context(nc.psum_tensor("side", [P, 2, TOK], F32))

        w_raw = sb("w_raw", [P, 3, WCOLS])
        w_hi = sb("w_hi", [P, NE, WCOLS], F32R)
        w_lo = sb("w_lo", [P, NE, WCOLS], F32R)
        router = sb("router", [P, KD, E])
        router_hl = sb("router_hl", [P, KD, 2 * E], F32R)
        rmsw = sb("rmsw", [P, KD])
        cst = sb("cst", [P, C_STAY])
        sel = sb("sel", [4 * HEADS, 2 * P], F32R)
        qk_hi = sb("qk_hi", [P, 2, KD, D], F32R)
        qk_lo = sb("qk_lo", [P, 2, KD, D], F32R)
        wo_hi = sb("wo_hi", [P, 2, D], F32R)
        wo_lo = sb("wo_lo", [P, 2, D], F32R)

        x_next = sb("x_next", [P, NT, D])
        x_in = sb("x_in", [P, NT, D])
        x_mid = sb("x_mid", [P, NT, D])
        x_last = sb("x_last", [P, NT, D])
        xn = {k: sb(f"xn{k}", [P, NT, D]) for k in ("_next", "")}
        stats = {k: sb(f"stats{k}", [P, NT, 6]) for k in "1A2"}
        mv = {k: sb(f"mv{k}", [P, NT, 2]) for k in "1A2"}
        scl = {k: sb(f"scl{k}", [P, 8, NT]) for k in "1A2"}
        half = sb("half", [P, NT])

        h_hi = {k: sb(f"h{k}_hi", [P, KD, TOK], F32R) for k in "1A2"}
        h_lo = {k: sb(f"h{k}_lo", [P, KD, TOK], F32R) for k in "1A2"}
        act = sb("act", [P, 3, TOK])
        act_hi = sb("act_hi", [P, 3, TOK], F32R)
        act_lo = sb("act_lo", [P, 3, TOK], F32R)

        lg2 = sb("lg2", [P, NT, 2 * E])
        lg = sb("lg", [P, NT, E])
        top8 = sb("top8", [P, NT, E])
        top_at = sb("top_at", [P, NT, E], mybir.dt.uint32)
        onehot = sb("onehot", [P, 2, NT, E])
        share = sb("share", [P, 2, NT, E])
        rt = sb("rt", [P, 4, NT])
        wt = sb("wt", [P, E, NT])
        wT = sb("wT", [E * NT, P])
        wrow = sb("wrow", [1, E * TOK])
        wb = sb("wb", [P, E, TOK])

        q_sb = sb("q_sb", [P, 2, TOK])
        k_sb = sb("k_sb", [P, 2, TOK])
        sq_q = sb("sq_q", [P, 2, TOK])
        sq_k = sb("sq_k", [P, 2, TOK])
        nrm = sb("nrm", [P, 4, P])
        inv = sb("inv", [P, NT, 2, 2 * HEADS], F32R)
        invT = sb("invT", [4 * HEADS, TOK], F32R)
        carry = sb("carry", [P, 2, 2 * PER_SEQ + 2])
        q_root = sq_q[:, 0]
        o_sb = sq_q
        o_hi = sb("o_hi", [P, 2, TOK], F32R)
        o_lo = sb("o_lo", [P, 2, TOK], F32R)
        wq_raw, wk_raw, wo_raw, woT = q_sb, k_sb, sq_q, sq_k
        dft, sel_raw = q_sb[:, :, D:], k_sb[0:4 * HEADS, 0, D:]

        ident = cst[:, C_ID:C_ID + P]
        one = cst[:, C_ONE:C_ONE + 1]

        gate_done, up_done, down_done, silu_done = sem("gate_done"), sem("up_done"), sem("down_done"), sem("silu_done")
        prod_done, weighted, act_hi_done, act_lo_done = sem("prod_done"), sem("weighted"), sem("act_hi_done"), sem("act_lo_done")
        y_read, side_full, side_read = sem("y_read"), sem("side_full"), sem("side_read")
        norm_v_done = sem("norm_v_done")
        stats_done, scale_done, norm_done, hi_done = sem("stats_done"), sem("scale_done"), sem("norm_done"), sem("hi_done")
        diff_done, tanh_done, wt_done = sem("diff_done"), sem("tanh_done"), sem("wt_done")
        wrow_in, wb_done = sem("wrow_in"), sem("wb_done")
        x_next_in, x_in_done, x1_done, x2_done = sem("x_next_in"), sem("x_in_done"), sem("x1_done"), sem("x2_done")
        x3_done, x_last_done, stored = sem("x3_done"), sem("x_last_done"), sem("stored")
        squared, sq_summed, inv_done, cum_done = sem("squared"), sem("sq_summed"), sem("inv_done"), sem("cum_done")
        q_root_done, q_scaled, k_scaled = sem("q_root_done"), sem("q_scaled"), sem("k_scaled")
        cross_done, o_done, o_hi_done, o_lo_done = sem("cross_done"), sem("o_done"), sem("o_hi_done"), sem("o_lo_done")
        w_hi_done, w_lo_done, cst_in, small_in = sem("w_hi_done"), sem("w_lo_done"), sem("cst_in"), sem("small_in")
        attn_w_in, router_hi_done, router_split, filled = sem("attn_w_in"), sem("router_hi_done"), sem("router_split"), sem("filled")
        sel_done = sem("sel_done")
        carried, dve_step, pool_step = sem("carried"), sem("dve_step"), sem("pool_step")
        raw_in = [sem(f"raw_in{r}") for r in range(3)]

        def positive(value):
            return type(value) is not int or value > 0

        def carry_wait(eng):
            eng.sem_inc(carried, 1)

        class Steps:

            def __init__(self, eng, sem, name):
                self.eng, self.sem, self.name, self.base, self.k = eng, sem, name, 0, 0

            def at(self, base):
                self.base, self.k = base, 0

            def link(self, ins):
                ins.then_inc(self.sem, 1)
                self.k += 1
                self.eng.wait_ge(self.sem, self.base + self.k)

        def ffn_no(i, window):
            return 2 * i if window == "A" else 2 * i + 1

        def run_periods(eng, window, counted=()):
            def measured(i):
                before = [c.k for c in counted]
                window(i, "A")
                window(i, "B")
                return [c.k - b for c, b in zip(counted, before)]

            measured(0)
            starts = [c.base + c.k for c in counted]
            with eng.Fori(1, LAST) as i:
                for c, s in zip(counted, starts):
                    c.at((i - 1) * STEPS[c.name] + s)
                per = measured(i)
                assert per == [STEPS[c.name] for c in counted], per
            for c, s in zip(counted, starts):
                c.at(s + STEPS[c.name] * (LAST - 1))
            measured(LAST)

        STEPS = {"dve_step": 28, "pool_step": 6}

        def route_no(i, name):
            if type(i) is int and i == -1:
                return 0
            if name[-1] == "1":
                return 2 * i + 1
            if name[-1] == "0":
                return 2 * i
            return 2 * i + 2 - (type(i) is int and i == LAST)

        def sum_no(i, name):
            if type(i) is int and i in (0, GROUPS):
                return 0 if i == 0 else 2 * GROUPS - 1
            return 2 * i - 1 if name[-1] == "1" else 2 * i

        def unfinished(f):
            return not (type(f) is int and f in (0, 2 * GROUPS - 1))

        def h_kind(i, w):
            return "1" if w == "B" and not (type(i) is int and i == LAST) else "2"

        def xn_of(s):
            return xn["_next" if s[-1] == "1" else ""]

        def turned(i, s):
            return "2" if type(i) is int and i == -1 else s[-1]

        block = ctx.enter_context(nc.Block())

        @block.sync
        def _(sp):
            def load_expert(e):
                if e >= 3:
                    sp.wait_ge(w_lo_done, e - 2)
                g, u, d = (sw_gate, sw_up, sw_down) if e == 0 else (w_gate[e - 1], w_up[e - 1], w_down[e - 1])
                r = e % 3
                sp.dma_start(w_raw[:, r, WG:WU].rearrange("p (k f) -> p k f", k=KD),
                             g.rearrange("(k p) f -> p k f", p=P)).then_inc(raw_in[r], 16)
                sp.dma_start(w_raw[:, r, WU:WD].rearrange("p (k f) -> p k f", k=KD),
                             u.rearrange("(k p) f -> p k f", p=P)).then_inc(raw_in[r], 16)
                sp.dma_start(w_raw[:, r, WD:], d).then_inc(raw_in[r], 16)

            def load_x(g):
                sp.dma_start(x_next[:], x_rows[bass.ds(g * TOK, TOK), :].rearrange("(t p) d -> p t d", p=P)
                             ).then_inc(x_next_in, 16)

            def stage(s, i):
                if s == "loadx":
                    sp.wait_ge(x_in_done, i + 1)
                    carry_wait(sp)
                    sp.wait_ge(norm_done, norm_no(i - 1, "norm1", GROUPS) + 1)
                    carry_wait(sp)
                    sp.wait_ge(norm_v_done, norm_no(i - 1, "norm1", GROUPS) + 1)
                    carry_wait(sp)
                    load_x(i + 1)
                if s in ("wrow0", "wrow1", "wrow2"):
                    sp.wait_ge(side_read, side_no(i, s, GROUPS) + 1)
                    carry_wait(sp)
                    if positive(E * route_no(i, s)):
                        sp.wait_ge(wb_done, E * route_no(i, s))
                    carry_wait(sp)
                    sp.dma_start(wrow[:, :], wT[:, :]).then_inc(wrow_in, 16)
                if s == "sum2":
                    sp.wait_ge(x3_done, i)
                    carry_wait(sp)
                    sp.dma_start(out_rows[bass.ds((i - 1) * TOK, TOK), :].rearrange("(t p) d -> p t d", p=P),
                                 x_last[:]).then_inc(stored, 16)

            load_x(0)
            sp.dma_start(cst[:], consts[:, 0:C_STAY]).then_inc(cst_in, 16)
            sp.dma_start(rmsw[:], rms_weight.rearrange("(k p) -> p k", p=P), allow_slow_non_contiguous=True).then_inc(small_in, 16)
            sp.dma_start(router[:], router_w.rearrange("(k p) e -> p k e", p=P)).then_inc(small_in, 16)
            for e in range(3):
                load_expert(e)
            for dst, src in ((wq_raw, W_q), (wk_raw, W_kv), (wo_raw, W_o)):
                sp.dma_start(dst[:, :, 0:D], src.rearrange("(k p) d -> p k d", p=P)).then_inc(attn_w_in, 16)
            sp.dma_start(dft, consts[:, C_DFT:C_SELB].rearrange("p (k d) -> p k d", k=KD)).then_inc(attn_w_in, 16)
            sp.dma_start(sel_raw, consts[0:4 * HEADS, C_SELB:]).then_inc(attn_w_in, 16)
            stage("loadx", 0)
            for e in range(3, NE):
                load_expert(e)
                if e == 5:
                    stage("wrow1", -1)
            stage("wrow1", 0)

            def window(i, w):
                for before, after in stages(i, w, GROUPS):
                    for s in before + after:
                        stage(s, i)

            run_periods(sp, window)
            stage("sum2", GROUPS)
            sp.wait_ge(stored, 16 * GROUPS)

        @block.tensor
        def _(pe):
            def triple(dst, a, b, start, stop):
                (ah, al), (bh, bl) = a, b
                nc.tensor.matmul(dst, ah, bh, start=start, stop=False, skip_group_check=True)
                nc.tensor.matmul(dst, ah, bl, start=False, stop=False, skip_group_check=True)
                return nc.tensor.matmul(dst, al, bh, start=False, stop=stop, skip_group_check=True)

            def keep_warm(name):
                for _ in range(WARM[name]):
                    nc.tensor.transpose(gate_ps[:, 1, 0:P], ident, ident)

            def gate_up(f, e, kind):
                n = NE * f + e
                if type(f) is int and f == 0:
                    pe.wait_ge(w_hi_done, e + 1)
                    pe.wait_ge(w_lo_done, e + 1)
                last = n - (1 if e == 0 else 3 if e == 1 else 2)
                if positive(last + 1):
                    pe.wait_ge(silu_done, last + 1)
                for k in range(KD):
                    c = slice(WG + k * F, WG + (k + 1) * F)
                    ins = triple(gate_ps[:, e % 2], (w_hi[:, e, c], w_lo[:, e, c]),
                                 (h_hi[kind][:, k], h_lo[kind][:, k]), k == 0, k == KD - 1)
                ins.then_inc(gate_done, 1)
                if positive(last + 1):
                    pe.wait_ge(prod_done, last + 1)
                for k in range(KD):
                    c = slice(WU + k * F, WU + (k + 1) * F)
                    ins = triple(up_ps[:, e % 2], (w_hi[:, e, c], w_lo[:, e, c]),
                                 (h_hi[kind][:, k], h_lo[kind][:, k]), k == 0, k == KD - 1)
                ins.then_inc(up_done, 1)

            def down(f, e):
                n = NE * f + e
                pe.wait_ge(act_lo_done, n + 1)
                if e == 0:
                    if positive(f):
                        pe.wait_ge(y_read, f)
                for t in range(NT):
                    c = slice(t * P, (t + 1) * P)
                    ins = triple(y_ps[:, t], (act_hi[:, e % 3, c], act_lo[:, e % 3, c]),
                                 (w_hi[:, e, WD:], w_lo[:, e, WD:]), e == 0 and t % 2 == 0, e == NE - 1)
                ins.then_inc(down_done, 1)

            def stage(s, i):
                if s in SIDE:
                    u = side_no(i, s, GROUPS)
                    if s in ("turn1", "turnA", "turn2"):
                        pe.wait_ge(norm_done, norm_no(i, "norm" + s[-1], GROUPS) + 1)
                        pe.wait_ge(norm_v_done, norm_no(i, "norm" + s[-1], GROUPS) + 1)
                    if s in ("wrow0", "wrow1", "wrow2"):
                        pe.wait_ge(wt_done, route_no(i, s) + 1)
                    if s == "sq":
                        pe.wait_ge(sq_summed, 2 * i + 2)
                    if s == "inv":
                        pe.wait_ge(inv_done, i + 1)
                    if s == "spread" and type(i) is int and i == 0:
                        pe.wait_ge(sel_done, 1)
                    if s == "wo":
                        pe.wait_ge(o_lo_done, 2 * i + 1)
                    if positive(u):
                        pe.wait_ge(side_read, u)
                if s in ("turn1", "turnA", "turn2"):
                    for k in range(KD):
                        for t in range(NT):
                            ins = nc.tensor.transpose(side[:, k, t * P:(t + 1) * P],
                                                      xn_of(s)[:, t, k * P:(k + 1) * P], ident)
                elif s in ("route1", "route2"):
                    hh, hl = h_hi[turned(i, s)], h_lo[turned(i, s)]
                    for t in range(NT):
                        for k in range(KD):
                            for part in (hh, hl):
                                ins = nc.tensor.matmul(side[:, 0, t * 2 * E:(t + 1) * 2 * E],
                                                       part[:, k, t * P:(t + 1) * P], router_hl[:, k],
                                                       start=k == 0 and part is hh, stop=k == KD - 1 and part is hl,
                                                       skip_group_check=True)
                elif s in ("wrow0", "wrow1", "wrow2"):
                    ins = nc.tensor.transpose(side[0:E * NT, 1, 0:P], wt[:].rearrange("p e t -> p (e t)"), ident)
                elif s in ("q", "k"):
                    j = "qk".index(s)
                    for plane in range(2):
                        for k in range(KD):
                            c = slice(plane * P, (plane + 1) * P)
                            ins = triple(side[:, plane], (qk_hi[:, j, k, c], qk_lo[:, j, k, c]),
                                         (h_hi["A"][:, k], h_lo["A"][:, k]), k == 0, k == KD - 1)
                elif s == "sq":
                    for t in range(NT):
                        dst = side[:, 0, 2 * HEADS * t:2 * HEADS * (t + 1)]
                        c = slice(t * P, (t + 1) * P)
                        nc.tensor.matmul(dst, sq_q[:, 0, c], cst[:, C_SELN:C_SELN + 32],
                                         start=True, stop=False, skip_group_check=True)
                        ins = nc.tensor.matmul(dst, sq_k[:, 0, c], cst[:, C_SELN + 32:C_SELN + 64],
                                               start=False, stop=True, skip_group_check=True)
                elif s == "inv":
                    carry_wait(pe)
                    for t in range(NT):
                        ins = nc.tensor.transpose(side[0:4 * HEADS, 1, t * P:(t + 1) * P],
                                                  inv[:, t].rearrange("p a b -> p (a b)").bitcast(F32), ident)
                elif s == "spread":
                    for j in range(2):
                        ins = nc.tensor.matmul(side[:, j], sel[:, j * P:(j + 1) * P], invT[:], start=True, stop=True)
                elif s == "wo":
                    for plane in range(2):
                        if plane == 1:
                            pe.wait_ge(o_lo_done, 2 * i + 2)
                        for t in range(NT):
                            c = slice(t * P, (t + 1) * P)
                            ins = triple(side[:, t // 2, (t % 2) * D:(t % 2 + 1) * D], (o_hi[:, plane, c], o_lo[:, plane, c]),
                                         (wo_hi[:, plane], wo_lo[:, plane]),
                                         plane == 0 and t % 2 == 0, plane == 1)
                else:
                    if s == "end7":
                        down(ffn_no(i, "A"), NE - 2)
                    if s == "end8":
                        down(ffn_no(i, "A"), NE - 1)
                    if s in WARM:
                        pe.wait_ge(silu_done, NE * ffn_no(i, "B" if i == 0 else "A") + NE - 1)
                        keep_warm(s)
                    return
                ins.then_inc(side_full, 1)

            def fold(name, raw):
                pe.wait_ge(side_read, SETUP_SIDE.index(name))
                pe.wait_ge(attn_w_in, 80)
                for m in range(KD):
                    for k in range(KD):
                        ins = nc.tensor.matmul(side[:, m, 0:D], raw[:, k, m * P:(m + 1) * P],
                                               dft[:, k],
                                               start=k == 0, stop=k == KD - 1)
                ins.then_inc(side_full, 1)

            def turn_wo():
                pe.wait_ge(side_read, SETUP_SIDE.index("woT"))
                for m in range(KD):
                    for k in range(KD):
                        ins = nc.tensor.transpose(side[:, m, k * P:(k + 1) * P],
                                                  wo_raw[:, k, m * P:(m + 1) * P], ident)
                ins.then_inc(side_full, 1)

            def fold_wo():
                pe.wait_ge(side_read, SETUP_SIDE.index("wo"))
                for plane in range(2):
                    for k in range(KD):
                        ins = nc.tensor.matmul(side[:, plane, 0:D], dft[:, k, plane * P:(plane + 1) * P], woT[:, k, 0:D],
                                               start=k == 0, stop=k == KD - 1)
                ins.then_inc(side_full, 1)

            pe.wait_ge(cst_in, 16)
            keep_warm("warm_start")
            stage("turn1", -1)
            keep_warm("warm_split")
            pe.wait_ge(router_split, 1)
            stage("route1", -1)
            for e in range(NE):
                before, after = STAGES_SETUP[e]
                gate_up(0, e, "2")
                for s in before:
                    if s == "wo":
                        fold_wo()
                    else:
                        stage(s, -1 if e == 1 else 0)
                if e >= 2:
                    down(0, e - 2)
                for s in after:
                    if s == "wq":
                        fold("wq", wq_raw)
                    elif s == "wk":
                        fold("wk", wk_raw)
                    elif s == "woT":
                        turn_wo()
                    else:
                        stage(s, 0)

            def window(i, w):
                f = ffn_no(i, w)
                for e, (before, after) in enumerate(stages(i, w, GROUPS)):
                    if e < NE:
                        gate_up(f, e, h_kind(i, w))
                    for s in before:
                        stage(s, i)
                    if e < 2 and unfinished(f):
                        down(f - 1, NE - 2 + e)
                    elif 2 <= e < NE:
                        down(f, e - 2)
                    for s in after:
                        stage(s, i)

            run_periods(pe, window)
            down(2 * GROUPS - 1, NE - 2)
            down(2 * GROUPS - 1, NE - 1)

        @block.scalar
        def _(act_e):
            A = nc.scalar

            def silu(f, e):
                n = NE * f + e
                act_e.wait_ge(gate_done, n + 1)
                if positive(n - 2):
                    act_e.wait_ge(act_lo_done, n - 2)
                A.activation(act[:, e % 3], gate_ps[:, e % 2], ACT.Silu).then_inc(silu_done, 1)

            def high(f, e):
                n = NE * f + e
                if e == 0:
                    act_e.wait_ge(prod_done, n + 1)
                else:
                    act_e.wait_ge(weighted, E * f + e)
                if positive(n - 2):
                    act_e.wait_ge(down_done, n - 2)
                A.activation(act_hi[:, e % 3], act[:, e % 3], ACT.Copy).then_inc(act_hi_done, 1)

            def core(f, e):
                silu(f, e)
                if e >= 1:
                    high(f, e - 1)
                elif unfinished(f):
                    high(f - 1, NE - 1)

            def stage(s, i):
                full = side_no(i, s, GROUPS) + 1 if s in SIDE else None
                if s in NORMS:
                    src, kind = (x_next if s == "norm1" else x_mid), s[-1]
                    act_e.wait_ge(scale_done, norm_no(i, s, GROUPS) + 1)
                    for t in range(NT // 2):
                        ins = A.activation(xn_of(s)[:, t], src[:, t], ACT.Identity, bias=scl[kind][:, 6, t:t + 1],
                                           scale=scl[kind][:, 7, t:t + 1])
                    ins.then_inc(norm_done, 1)
                elif s in ("turn1", "turnA", "turn2"):
                    kind = turned(i, s)
                    act_e.wait_ge(side_full, full)
                    for k in range(KD):
                        if kind == "A":
                            ins = A.activation(h_hi[kind][:, k], side[:, k], ACT.Copy)
                        else:
                            ins = A.activation(h_hi[kind][:, k], side[:, k], ACT.Copy, scale=rmsw[:, k:k + 1])
                        ins.then_inc(hi_done, 1)
                elif s in ("gatew1", "gatew2"):
                    act_e.wait_ge(diff_done, route_no(i, s) + 1)
                    A.activation(rt[:, 1], rt[:, 0], ACT.Tanh, scale=0.5).then_inc(tanh_done, 1)
                elif s in ("wrow0", "wrow1", "wrow2"):
                    act_e.wait_ge(side_full, full)
                    if positive(16 * route_no(i, s)):
                        act_e.wait_ge(wrow_in, 16 * route_no(i, s))
                    A.copy(wT[:, :], side[0:E * NT, 1, 0:P]).then_inc(side_read, 1)
                elif s == "end8":
                    high(ffn_no(i, "A"), NE - 1)
                elif s == "xa":
                    act_e.wait_ge(x1_done, i + 1)
                    act_e.wait_ge(x_next_in, 16 * (i + 2))
                    A.copy(x_in[:], x_next[:]).then_inc(x_in_done, 1)
                elif s == "xc":
                    act_e.wait_ge(x2_done, i + 1)
                    if positive(16 * i):
                        act_e.wait_ge(stored, 16 * i)
                    A.copy(x_last[:], x_mid[:]).then_inc(x_last_done, 1)
                elif s in ("q", "k"):
                    act_e.wait_ge(side_full, full)
                    sq, dst = (sq_q, q_sb) if s == "q" else (sq_k, k_sb)
                    A.activation(sq[:], side[:], ACT.Square).then_inc(squared, 1)
                    A.copy(dst[:], side[:]).then_inc(side_read, 1)
                elif s == "inv":
                    act_e.wait_ge(side_full, full)
                    A.copy(invT[:, :], side[0:4 * HEADS, 1, :]).then_inc(side_read, 1)
                elif s == "spread":
                    act_e.wait_ge(side_full, full)
                    A.copy(q_root, side[:, 0]).then_inc(q_root_done, 1)
                elif s == "osplit":
                    for plane in range(2):
                        act_e.wait_ge(o_done, 2 * i + 1 + plane)
                        A.activation(o_hi[:, plane], o_sb[:, plane], ACT.Copy).then_inc(o_hi_done, 1)

            def split_expert(e):
                act_e.wait_ge(raw_in[e % 3], 48 * (e // 3 + 1))
                A.activation(w_hi[:, e], w_raw[:, e % 3], ACT.Copy).then_inc(w_hi_done, 1)

            def setup_high(name, dst, scale):
                act_e.wait_ge(side_full, SETUP_SIDE.index(name) + 1)
                A.activation(dst, side[:, :, 0:D], ACT.Copy, scale=scale).then_inc(hi_done, 1)

            act_e.wait_ge(small_in, 32)
            A.activation(router_hl[:, :, 0:E], router[:], ACT.Copy).then_inc(router_hi_done, 1)
            split_expert(0)
            act_e.wait_ge(x_next_in, 16)
            stage("norm1", -1)
            A.copy(x_in[:], x_next[:]).then_inc(x_in_done, 1)
            stage("turn1", -1)
            split_expert(1)
            for e in range(NE):
                core(0, e)
                if e == 0:
                    stage("gatew1", -1)
                if e == 1:
                    stage("wrow1", -1)
                if e + 2 < NE:
                    split_expert(e + 2)
                before, after = STAGES_SETUP[e]
                for s in before + after:
                    if s == "wq":
                        setup_high("wq", qk_hi[:, 0], 1.0)
                    elif s == "wk":
                        setup_high("wk", qk_hi[:, 1], 1.0)
                    elif s == "woT":
                        act_e.wait_ge(side_full, SETUP_SIDE.index("woT") + 1)
                        A.copy(woT[:, :, 0:D], side[:, :, 0:D]).then_inc(side_read, 1)
                        A.copy(sel[:, :], sel_raw).then_inc(sel_done, 1)
                    elif s == "wo":
                        setup_high("wo", wo_hi[:], CONV_SCALE)
                    elif s == "loadx" or e > 1:
                        stage(s, 0)

            def window(i, w):
                f = ffn_no(i, w)
                for e, (before, after) in enumerate(stages(i, w, GROUPS)):
                    if e < NE:
                        core(f, e)
                    for s in before + after:
                        stage(s, i)

            run_periods(act_e, window)
            high(2 * GROUPS - 1, NE - 1)

        @block.vector
        def _(dve):
            V = nc.vector
            step = Steps(dve, dve_step, "dve_step")
            link = step.link

            def product(f, e):
                n = NE * f + e
                dve.wait_ge(silu_done, n + 1)
                dve.wait_ge(up_done, n + 1)
                V.tensor_tensor(act[:, e % 3], act[:, e % 3], up_ps[:, e % 2], ALU.mult).then_inc(prod_done, 1)

            def weigh(f, e):
                dve.wait_ge(prod_done, NE * f + e + 1)
                dve.wait_ge(wb_done, E * f + e)
                V.tensor_tensor(act[:, e % 3], act[:, e % 3], wb[:, e - 1], ALU.mult).then_inc(weighted, 1)

            def low(f, e):
                n = NE * f + e
                dve.wait_ge(act_hi_done, n + 1)
                if positive(n - 2):
                    dve.wait_ge(down_done, n - 2)
                V.tensor_tensor(act_lo[:, e % 3], act[:, e % 3], act_hi[:, e % 3].bitcast(F32),
                                ALU.subtract).then_inc(act_lo_done, 1)

            def core(f, e):
                product(f, e)
                if e >= 1:
                    low(f, e - 1)
                elif unfinished(f):
                    low(f - 1, NE - 1)
                if e >= 1:
                    weigh(f, e)

            def newton():
                n2, y, t = (nrm[:, j] for j in range(3))
                link(V.tensor_tensor(t, y, y, ALU.mult))
                link(V.scalar_tensor_tensor(out=t, in0=t, scalar=-0.5, in1=n2, op0=ALU.mult, op1=ALU.mult))
                link(V.scalar_tensor_tensor(out=y, in0=t, scalar=1.5, in1=y, op0=ALU.add, op1=ALU.mult))

            def rows(tile):
                return tile[:].rearrange("p t d -> p (t d)")

            def stage(s, i):
                u = side_no(i, s, GROUPS) if s in SIDE else None
                if s in SIDE and s not in ("wrow0", "wrow1", "wrow2", "q", "k", "inv"):
                    dve.wait_ge(side_full, u + 1)
                if s in ("stat1", "statA", "stat2"):
                    src = x_next if s == "stat1" else x_mid
                    if s == "stat1":
                        dve.wait_ge(x_next_in, 16 * (i + 2))
                    for t in range(NT):
                        ins = V.bn_stats(stats[s[-1]][:, t], src[:, t])
                    link(ins)
                    carry_wait(dve)
                    for t in range(NT):
                        ins = V.bn_aggr(mv[s[-1]][:, t], stats[s[-1]][:, t])
                    ins.then_inc(stats_done, 1)
                elif s in NORMS:
                    src, kind = (x_next if s == "norm1" else x_mid), s[-1]
                    dve.wait_ge(scale_done, norm_no(i, s, GROUPS) + 1)
                    carry_wait(dve)
                    for t in range(NT // 2, NT):
                        ins = V.tensor_scalar(xn_of(s)[:, t], src[:, t], scl[kind][:, 7, t:t + 1],
                                              scl[kind][:, 6, t:t + 1], ALU.mult, ALU.add)
                    ins.then_inc(norm_v_done, 1)
                elif s in ("turn1", "turnA", "turn2"):
                    kind = turned(i, s)
                    for k in range(KD):
                        n = norm_no(i, "norm" + s[-1], GROUPS)
                        dve.wait_ge(hi_done, 2 * n + k + 1 + (0 if type(i) is int and i == -1 else 3))
                        hi = h_hi[kind][:, k].bitcast(F32)
                        if kind == "A":
                            ins = V.tensor_tensor(h_lo[kind][:, k], side[:, k], hi, ALU.subtract)
                        else:
                            ins = V.scalar_tensor_tensor(out=h_lo[kind][:, k], in0=side[:, k], scalar=rmsw[:, k:k + 1],
                                                         in1=hi, op0=ALU.mult, op1=ALU.subtract)
                    ins.then_inc(side_read, 1)
                elif s in ("route1", "route2"):
                    V.tensor_copy(lg2[:].rearrange("p t e -> p (t e)"), side[:, 0, 0:NT * 2 * E]).then_inc(side_read, 1)
                    dve.wait_ge(side_read, u + 1)
                    link(V.tensor_tensor(lg[:], lg2[:, :, 0:E], lg2[:, :, E:], ALU.add))
                    carry_wait(dve)
                    for t in range(NT):
                        ins = V.max(top8[:, t], lg[:, t])
                    link(ins)
                    carry_wait(dve)
                    for t in range(NT):
                        ins = V.max_index(top_at[:, t], top8[:, t], lg[:, t])
                    link(ins)
                    for j in range(2):
                        V.tensor_tensor(onehot[:, j], cst[:, C_INDEX:C_INDEX + E].unsqueeze(1).broadcast_to([P, NT, E]),
                                        top_at[:, :, j:j + 1].broadcast_to([P, NT, E]), ALU.is_equal)
                    V.tensor_tensor(rt[:, 0], top8[:, :, 1], top8[:, :, 0], ALU.subtract).then_inc(diff_done, 1)
                elif s in ("gatew1", "gatew2"):
                    dve.wait_ge(tanh_done, route_no(i, s) + 1)
                    V.tensor_scalar(rt[:, 2], rt[:, 1], -0.5, 0.5, ALU.mult, ALU.add)
                    link(V.tensor_scalar(rt[:, 3], rt[:, 1], 0.5, 0.5, ALU.mult, ALU.add))
                    link(V.tensor_tensor(share[:], onehot[:], rt[:, 2:4].unsqueeze(3).broadcast_to([P, 2, NT, E]),
                                         ALU.mult))
                    V.tensor_tensor(wt[:].rearrange("p e t -> p t e"), share[:, 0], share[:, 1],
                                    ALU.add).then_inc(wt_done, 1)
                elif s == "end8":
                    low(ffn_no(i, "A"), NE - 1)
                elif s == "sum1":
                    dve.wait_ge(down_done, NE * (sum_no(i, s) + 1))
                    dve.wait_ge(x_in_done, i + 1)
                    if positive(i):
                        dve.wait_ge(x_last_done, i)
                    V.scalar_tensor_tensor(out=rows(x_mid), in0=rows(y_ps), scalar=0.5, in1=rows(x_in),
                                           op0=ALU.mult, op1=ALU.add).then_inc(x1_done, 1)
                    dve.wait_ge(x1_done, i + 1)
                    dve.sem_inc(y_read, 1)
                elif s == "sum2":
                    dve.wait_ge(down_done, NE * (sum_no(i, s) + 1))
                    dve.wait_ge(x_last_done, i)
                    V.scalar_tensor_tensor(out=rows(x_last), in0=rows(y_ps), scalar=0.5, in1=rows(x_last),
                                           op0=ALU.mult, op1=ALU.add).then_inc(x3_done, 1)
                    dve.wait_ge(x3_done, i)
                    dve.sem_inc(y_read, 1)
                elif s == "wo":
                    V.tensor_tensor(rows(x_mid), side[:].rearrange("p b c -> p (b c)"), rows(x_mid), ALU.add
                                    ).then_inc(x2_done, 1)
                    dve.wait_ge(x2_done, i + 1)
                    dve.sem_inc(side_read, 1)
                elif s == "sq":
                    n2, y, t, zero = (nrm[:, j] for j in range(4))
                    V.tensor_copy(n2, side[:, 0, 0:P]).then_inc(side_read, 1)
                    dve.wait_ge(side_read, u + 1)
                    link(V.tensor_scalar(t.bitcast(I32), n2.bitcast(I32), 1, None, ALU.logical_shift_right))
                    link(V.tensor_scalar(y.bitcast(I32), t.bitcast(I32), -1.0, float(RSQRT_MAGIC), ALU.mult, ALU.add))
                    V.tensor_scalar(zero, n2, 0.0, BIG, ALU.is_equal, ALU.mult)
                    newton()
                elif s == "sq2":
                    newton()
                    newton()
                    link(V.scalar_tensor_tensor(out=nrm[:, 1], in0=nrm[:, 3], scalar=BIG, in1=nrm[:, 1],
                                                op0=ALU.mult, op1=ALU.add))
                    root = nrm[:, 1].rearrange("p (t h) -> p t h", t=NT)
                    link(V.tensor_copy(inv[:, :, 0], root))
                    V.tensor_tensor(inv[:, :, 1], root, inv[:, :, 0].bitcast(F32), ALU.subtract).then_inc(inv_done, 1)
                elif s == "spread":
                    slot = (5 * i) >> 2
                    V.tensor_tensor(k_sb[:], k_sb[:], side[:, 1].unsqueeze(1).broadcast_to([P, 2, TOK]),
                                    ALU.mult).then_inc(k_scaled, 1)
                    dve.wait_ge(q_root_done, i + 1)
                    dve.wait_ge(k_scaled, i + 1)
                    dve.sem_inc(side_read, 1)
                    for plane in range(2):
                        ins = V.tensor_tensor_scan(k_sb[:, plane], one.broadcast_to([P, TOK]), k_sb[:, plane],
                                                   carry[:, plane, bass.ds(slot, 1)], ALU.mult, ALU.add)
                    link(ins)
                    V.tensor_copy(carry[:, :, bass.ds(slot + 1, 1)], k_sb[:, :, TOK - 1:TOK]).then_inc(cum_done, 1)
                elif s == "conv":
                    dve.wait_ge(q_scaled, i + 1)
                    V.tensor_tensor(sq_q[:], q_sb[:], k_sb[:], ALU.mult)
                    link(V.tensor_tensor(sq_k[:, 0], q_sb[:, 1], k_sb[:, 0], ALU.mult))
                elif s == "conv2":
                    V.scalar_tensor_tensor(out=o_sb[:, 0], in0=sq_q[:, 1], scalar=cst[:, C_SIGN:C_SIGN + 1],
                                           in1=sq_q[:, 0], op0=ALU.mult, op1=ALU.add).then_inc(o_done, 1)
                    dve.wait_ge(o_done, 2 * i + 1)
                    dve.wait_ge(cross_done, i + 1)
                    V.tensor_tensor(o_sb[:, 1], sq_k[:, 0], sq_k[:, 1], ALU.add).then_inc(o_done, 1)
                elif s == "osplit":
                    for plane in range(2):
                        dve.wait_ge(o_hi_done, 2 * i + 1 + plane)
                        V.tensor_tensor(o_lo[:, plane], o_sb[:, plane], o_hi[:, plane].bitcast(F32), ALU.subtract
                                        ).then_inc(o_lo_done, 1)

            def split_expert(e):
                dve.wait_ge(w_hi_done, e + 1)
                V.tensor_tensor(w_lo[:, e], w_raw[:, e % 3], w_hi[:, e].bitcast(F32),
                                ALU.subtract).then_inc(w_lo_done, 1)

            def setup_low(name, dst, hi, scale, count):
                dve.wait_ge(hi_done, count)
                V.scalar_tensor_tensor(out=dst, in0=side[:, :, 0:D], scalar=scale, in1=hi.bitcast(F32),
                                       op0=ALU.mult, op1=ALU.subtract).then_inc(side_read, 1)

            V.memset(carry[:], 0.0)
            V.memset(half[:], -0.5).then_inc(filled, 1)
            stage("stat1", -1)
            dve.wait_ge(cst_in, 16)
            dve.wait_ge(small_in, 32)
            dve.wait_ge(router_hi_done, 1)
            V.tensor_tensor(router_hl[:, :, E:], router[:], router_hl[:, :, 0:E].bitcast(F32), ALU.subtract
                            ).then_inc(router_split, 1)
            split_expert(0)
            stage("norm1", -1)
            stage("turn1", -1)
            stage("route1", -1)
            split_expert(1)
            for e in range(NE):
                if e == 1:
                    stage("gatew1", -1)
                core(0, e)
                if e + 2 < NE:
                    split_expert(e + 2)
                before, after = STAGES_SETUP[e]
                for s in before + after:
                    if s == "wq":
                        setup_low("wq", qk_lo[:, 0], qk_hi[:, 0], 1.0, 3)
                    elif s == "wk":
                        setup_low("wk", qk_lo[:, 1], qk_hi[:, 1], 1.0, 4)
                    elif s == "wo":
                        setup_low("wo", wo_lo[:], wo_hi[:], CONV_SCALE, 5)
                    elif s == "loadx" or e > 1:
                        stage(s, 0)

            def window(i, w):
                f = ffn_no(i, w)
                for e, (before, after) in enumerate(stages(i, w, GROUPS)):
                    if e < NE:
                        core(f, e)
                    for s in before + after:
                        stage(s, i)

            run_periods(dve, window, (step,))
            low(2 * GROUPS - 1, NE - 1)
            stage("sum2", GROUPS)

        @block.gpsimd
        def _(pool):
            G = nc.gpsimd
            step = Steps(pool, pool_step, "pool_step")
            link = step.link

            def stage(s, i):
                if s in ("stat1", "statA", "stat2"):
                    n = norm_no(i, "norm" + s[-1], GROUPS)
                    mean, var, scl_k = mv[s[-1]][:, :, 0], mv[s[-1]][:, :, 1], scl[s[-1]]
                    pool.wait_ge(stats_done, n + 1)
                    carry_wait(pool)
                    if s == "statA":
                        link(G.tensor_scalar(scl_k[:, 0], var, LN_EPS, None, ALU.add))
                    else:
                        link(G.tensor_scalar(scl_k[:, 0], var, 1.0 + RMS_EPS, LN_EPS * RMS_EPS, ALU.mult, ALU.add))
                    G.tensor_tensor(scl_k[:, 7], scl_k[:, 0], half[:], ALU.pow)
                    link(G.tensor_scalar(scl_k[:, 5], mean, -1.0, None, ALU.mult))
                    G.tensor_tensor(scl_k[:, 6], scl_k[:, 5], scl_k[:, 7], ALU.mult).then_inc(scale_done, 1)
                elif s in ("wspread0", "wspread1", "wspread2"):
                    r = route_no(i, s)
                    pool.wait_ge(wrow_in, 16 * (r + 1))
                    for e in range(E):
                        if not (type(i) is int and i == -1):
                            pool.wait_ge(weighted, E * (r - 1) + e + 1)
                        carry_wait(pool)
                        G.partition_broadcast(wb[:, e], wrow[0:1, e * TOK:(e + 1) * TOK], channels=P
                                              ).then_inc(wb_done, 1)
                elif s in ("q", "k"):
                    sq = sq_q if s == "q" else sq_k
                    pool.wait_ge(squared, 2 * i + 1 + (s == "k"))
                    G.tensor_tensor(sq[:, 0], sq[:, 0], sq[:, 1], ALU.add).then_inc(sq_summed, 1)
                elif s == "spread":
                    pool.wait_ge(q_root_done, i + 1)
                    G.tensor_tensor(q_sb[:], q_sb[:], q_root.unsqueeze(1).broadcast_to([P, 2, TOK]),
                                    ALU.mult).then_inc(q_scaled, 1)
                elif s == "conv":
                    pool.wait_ge(cum_done, i + 1)
                    pool.wait_ge(q_scaled, i + 1)
                    G.tensor_tensor(sq_k[:, 1], q_sb[:, 0], k_sb[:, 1], ALU.mult).then_inc(cross_done, 1)

            pool.wait_ge(filled, 1)
            stage("stat1", -1)
            stage("wspread1", -1)
            stage("stat1", 0)
            stage("wspread1", 0)

            def window(i, w):
                for before, after in stages(i, w, GROUPS):
                    for s in before + after:
                        stage(s, i)

            run_periods(pool, window, (step,))


_INS = ["L0_attn_x", "L0_attn_W_q", "L0_attn_W_kv", "L0_attn_W_o", "L0_ffn_rms_weight", "L0_ffn_router_w",
        "L0_ffn_w_gate", "L0_ffn_w_up", "L0_ffn_w_down", "L0_ffn_sw_gate", "L0_ffn_sw_up", "L0_ffn_sw_down"]


def kernel(**inputs):
    import concourse.bacc as bacc
    from concourse.bass_utils import run_bass_kernel_spmd

    nc = bacc.Bacc("TRN2", target_bir_lowering=False, num_devices=1)
    arrays = {name: np.ascontiguousarray(inputs[name]) for name in _INS}
    arrays["constants"] = constants()
    args = [nc.dram_tensor(n, a.shape, mybir.dt.from_np(a.dtype), kind="ExternalInput").ap()
            for n, a in arrays.items()]
    out = nc.dram_tensor("out", arrays["L0_attn_x"].shape, F32, kind="ExternalOutput").ap()
    build(nc, *args, out)
    r = run_bass_kernel_spmd(nc, [arrays], core_ids=[0])
    return r.results[0]["out"]
```
